# Optimizing a Trainium2 kernel written in Bass

```python
import numpy as np
import jax
import jax.numpy as jnp

def _softmax(x, axis=-1):
    return jax.nn.softmax(x, axis=axis)

def _gelu(x):
    return jax.nn.gelu(x, approximate=True)

def _silu(x):
    return jax.nn.silu(x)

def _sigmoid(x):
    return jax.nn.sigmoid(x)

def _layernorm(x, axis=-1, eps=1e-05):
    m = jnp.mean(x, axis=axis, keepdims=True)
    v = jnp.var(x, axis=axis, keepdims=True)
    return (x - m) / jnp.sqrt(v + eps)

def _scatter_add(tgt, idx, src, axis=0):
    return tgt.at[idx].add(src)

def _segment_sum(src, seg, n):
    return jax.ops.segment_sum(src, seg, n)
kernel_name = 'mk_pixart_resid_d1_seqx_r8_f84a0d'

def setup_inputs(seed: int=0):
    np.random.seed(seed)
    _w = jnp.asarray

    def _rec_inputs():
        import jax
        import jax.numpy as jnp
        _rk = jax.random.key(seed)
        x = -0.0002928 + 1 * jax.random.normal(jax.random.fold_in(_rk, 1), (16, 64, 256), jnp.float32)
        _lenS = 64 - jax.random.randint(jax.random.fold_in(_rk, 7), (16,), 0, max(1, 64 // 4) + 1, jnp.int32)
        _lenS2 = 64 - jax.random.randint(jax.random.fold_in(_rk, 8), (16,), 0, max(1, 64 // 4) + 1, jnp.int32)
        _ctx_2048P = jax.random.normal(jax.random.fold_in(_rk, 11), (16, 16, 256), jnp.float32)
        _ctx_2048c = jax.random.dirichlet(jax.random.fold_in(_rk, 511), 0.3 * jnp.ones((16,), jnp.float32), (16, 64))
        _ctx_2048t = jnp.einsum('bsk,bkd->bsd', _ctx_2048c, _ctx_2048P)
        _ctx_2048t = _ctx_2048t * jax.lax.rsqrt(jnp.mean(jnp.square(_ctx_2048t)) + 1e-12) * 0.953939
        ctx_2048 = -1.39393e-06 + 0.999914 * (_ctx_2048t + 0.3 * jax.random.normal(jax.random.fold_in(_rk, 611), (16, 64, 256), jnp.float32))
        itok_B_779_1933 = jax.random.randint(jax.random.fold_in(_rk, 12), (16,), 779, 1934, jnp.int32)
        return (x, ctx_2048, itok_B_779_1933)
    x, ctx_2048, itok_B_779_1933 = _rec_inputs()

    def _L0_xcond_setup():
        import jax, jax.numpy as jnp
        import numpy as np
        NUM_HEADS = 8
        HEAD_DIM = 64
        AVG_K_LENGTH = 20
        SCALE = 1.0 / (HEAD_DIM ** 0.5 * float(np.log(AVG_K_LENGTH)))
        key = jax.random.key(seed)
        k1, k2, k3, k4 = jax.random.split(key, 4)
        B, HD, LQ, LK = (4, NUM_HEADS * HEAD_DIM, 256, 256)
        q = jax.random.normal(k1, (B, HD, LQ), dtype=jnp.float32)
        k = jax.random.normal(k2, (B, HD, LK), dtype=jnp.float32)
        v = jax.random.normal(k3, (B, HD, LK), dtype=jnp.float32)
        k_length = jax.random.randint(k4, (B,), 64, LK + 1, dtype=jnp.int32)
        return {'q': q, 'k': k, 'v': v, 'k_length': k_length}
    _L0_xcond_all = _L0_xcond_setup()
    _L0_xcond_in = {k: v for k, v in _L0_xcond_all.items() if k in ()}
    del _L0_xcond_all

    def _L0_ffn_setup():
        import jax, jax.numpy as jnp
        import numpy as np
        import math
        B, S, D = (2, 128, 256)
        H, KVH, HD = (16, 4, 128)
        E, K, FF = (8, 2, 896)
        EPS = 1e-05
        ROPE_BASE = 1000000.0

        def rmsnorm(x, w, eps=EPS):
            xf = x.astype(jnp.float32)
            var = jnp.mean(xf * xf, axis=-1, keepdims=True)
            return (xf * jax.lax.rsqrt(var + eps)).astype(x.dtype) * w

        def apply_rope(x, cos, sin):
            x1 = x[..., 0::2]
            x2 = x[..., 1::2]
            r1 = x1 * cos - x2 * sin
            r2 = x1 * sin + x2 * cos
            return jnp.stack([r1, r2], axis=-1).reshape(x.shape)
        key = jax.random.key(seed)
        ks = jax.random.split(key, 12)
        sc = 0.02
        inp = {'x': jax.random.normal(ks[0], (B, S, D), jnp.float32), 'ln_w': jnp.ones((D,), jnp.float32), 'ff_ln_w': jnp.ones((D,), jnp.float32), 'wq': jax.random.normal(ks[1], (D, H * HD), jnp.float32) * sc, 'wk': jax.random.normal(ks[2], (D, KVH * HD), jnp.float32) * sc, 'wv': jax.random.normal(ks[3], (D, KVH * HD), jnp.float32) * sc, 'wo': jax.random.normal(ks[4], (H * HD, D), jnp.float32) * sc, 'gate_w': jax.random.normal(ks[5], (D, E), jnp.float32) * sc, 'w1': jax.random.normal(ks[6], (E, D, FF), jnp.float32) * sc, 'w3': jax.random.normal(ks[7], (E, D, FF), jnp.float32) * sc, 'w2': jax.random.normal(ks[8], (E, FF, D), jnp.float32) * sc}
        return inp
    _L0_ffn_all = _L0_ffn_setup()
    _L0_ffn_in = {k: v for k, v in _L0_ffn_all.items() if k in ('ln_w', 'ff_ln_w', 'wq', 'wk', 'wv', 'wo', 'gate_w', 'w1', 'w3', 'w2')}
    del _L0_ffn_all
    return {'x': x, 'ctx_2048': ctx_2048, 'itok_B_779_1933': itok_B_779_1933, 'L0_ffn_ln_w': _L0_ffn_in['ln_w'], 'L0_ffn_ff_ln_w': _L0_ffn_in['ff_ln_w'], 'L0_ffn_wq': _L0_ffn_in['wq'], 'L0_ffn_wk': _L0_ffn_in['wk'], 'L0_ffn_wv': _L0_ffn_in['wv'], 'L0_ffn_wo': _L0_ffn_in['wo'], 'L0_ffn_gate_w': _L0_ffn_in['gate_w'], 'L0_ffn_w1': _L0_ffn_in['w1'], 'L0_ffn_w3': _L0_ffn_in['w3'], 'L0_ffn_w2': _L0_ffn_in['w2']}

def reference(x, ctx_2048, itok_B_779_1933, L0_ffn_ln_w, L0_ffn_ff_ln_w, L0_ffn_wq, L0_ffn_wk, L0_ffn_wv, L0_ffn_wo, L0_ffn_gate_w, L0_ffn_w1, L0_ffn_w3, L0_ffn_w2):
    import jax
    import jax.numpy as jnp

    def _L0_xcond_ref(q, k, v, k_length):
        import jax, jax.numpy as jnp
        import numpy as np
        NUM_HEADS = 8
        HEAD_DIM = 64
        AVG_K_LENGTH = 20
        SCALE = 1.0 / (HEAD_DIM ** 0.5 * float(np.log(AVG_K_LENGTH)))
        b, hd, lq = q.shape
        lk = k.shape[-1]
        d = hd // NUM_HEADS
        qh = q.reshape(b, NUM_HEADS, d, lq)
        kh = k.reshape(b, NUM_HEADS, d, lk)
        vh = v.reshape(b, NUM_HEADS, d, lk)
        s = SCALE * jnp.log(k_length.astype(jnp.float32))[:, None, None, None]
        attn = jnp.einsum('bhdq,bhdk->bhqk', qh, kh)
        attn = jax.nn.softmax(s * attn, axis=-1)
        out = jnp.einsum('bhqk,bhdk->bhdq', attn, vh)
        return out.reshape(b, hd, lq)

    def _L0_ffn_ref(x, ln_w, ff_ln_w, wq, wk, wv, wo, gate_w, w1, w3, w2):
        import jax, jax.numpy as jnp
        import numpy as np
        import math
        B, S, D = (2, 128, 256)
        H, KVH, HD = (16, 4, 128)
        E, K, FF = (8, 2, 896)
        EPS = 1e-05
        ROPE_BASE = 1000000.0

        def rmsnorm(x, w, eps=EPS):
            xf = x.astype(jnp.float32)
            var = jnp.mean(xf * xf, axis=-1, keepdims=True)
            return (xf * jax.lax.rsqrt(var + eps)).astype(x.dtype) * w

        def apply_rope(x, cos, sin):
            x1 = x[..., 0::2]
            x2 = x[..., 1::2]
            r1 = x1 * cos - x2 * sin
            r2 = x1 * sin + x2 * cos
            return jnp.stack([r1, r2], axis=-1).reshape(x.shape)
        Bx, Sx, Dx = x.shape
        residual = x
        h = rmsnorm(x, ln_w)
        q = (h @ wq).reshape(Bx, Sx, H, HD)
        k = (h @ wk).reshape(Bx, Sx, KVH, HD)
        v = (h @ wv).reshape(Bx, Sx, KVH, HD)
        pos = jnp.arange(Sx, dtype=jnp.float32)
        inv_freq = ROPE_BASE ** (-jnp.arange(0, HD, 2, dtype=jnp.float32) / HD)
        ang = pos[:, None] * inv_freq[None, :]
        cos = jnp.cos(ang)[None, :, None, :]
        sin = jnp.sin(ang)[None, :, None, :]
        q = apply_rope(q, cos, sin)
        k = apply_rope(k, cos, sin)
        rep = H // KVH
        k = jnp.repeat(k, rep, axis=2)
        v = jnp.repeat(v, rep, axis=2)
        scores = jnp.einsum('bqhd,bkhd->bhqk', q, k) / math.sqrt(HD)
        causal = jnp.tril(jnp.ones((Sx, Sx), dtype=bool))
        scores = jnp.where(causal[None, None], scores, jnp.finfo(scores.dtype).min)
        attn = jax.nn.softmax(scores, axis=-1)
        o = jnp.einsum('bhqk,bkhd->bqhd', attn, v).reshape(Bx, Sx, H * HD)
        x = o @ wo + residual
        residual = x
        h = rmsnorm(x, ff_ln_w)
        ht = h.reshape(-1, Dx)
        logits = ht @ gate_w
        top_vals, top_idx = jax.lax.top_k(logits, K)
        gates = jax.nn.softmax(top_vals, axis=-1)
        out = jnp.zeros_like(ht)
        for e in range(E):
            we = jnp.sum(gates * (top_idx == e), axis=-1)
            ye = jax.nn.silu(ht @ w1[e]) * (ht @ w3[e]) @ w2[e]
            out = out + we[:, None] * ye
        return out.reshape(Bx, Sx, Dx) + residual
    x = x + _L0_xcond_ref(_layernorm(x, axis=-1), ctx_2048, ctx_2048, itok_B_779_1933)
    x = x + _L0_ffn_ref(_layernorm(x, axis=-1), L0_ffn_ln_w, L0_ffn_ff_ln_w, L0_ffn_wq, L0_ffn_wk, L0_ffn_wv, L0_ffn_wo, L0_ffn_gate_w, L0_ffn_w1, L0_ffn_w3, L0_ffn_w2)
    return x

_drawn_inputs = setup_inputs


def setup_inputs(seed=0):
    import zlib

    import numpy as np

    out = dict(_drawn_inputs(seed))
    spreads = {'L0_ffn_ln_w': (1.0, 0.6), 'L0_ffn_ff_ln_w': (1.0, 0.6)}
    factors = {'L0_ffn_wq': 8.0,
     'L0_ffn_wk': 8.0,
     'L0_ffn_gate_w': 6.306,
     'L0_ffn_w1': 5.651,
     'L0_ffn_w3': 5.579,
     'L0_ffn_w2': 5.598}
    for name, (base, spread) in spreads.items():
        noise = np.random.default_rng([zlib.crc32(name.encode()), seed]).standard_normal(out[name].shape)
        drawn = base * np.exp(spread * noise) if base else spread * noise
        out[name] = jnp.asarray(drawn.astype(out[name].dtype))
    for name, factor in factors.items():
        out[name] = (out[name] * factor).astype(out[name].dtype)
    return out
```

```python
from contextlib import ExitStack
import math

import concourse.bass as bass
from concourse import mybir

F32 = mybir.dt.float32
F32R = mybir.dt.float32r
I32 = mybir.dt.int32
ALU = mybir.AluOpType
ACT = mybir.ActivationFunctionType
AX = mybir.AxisListType
U32 = mybir.dt.uint32

P = 128
B, S, D = 16, 64, 256
NP = B // 2
AH, AD = 8, 8
J, HH = 4, 2
TERMS = 3
KR = 1 + TERMS * AD
H, KVH, HD = 16, 4, 128
KT = D // P
GROUPS = H // KVH + 1
QKV = (H + 2 * KVH) * HD
B_SCALE = 1.0 / math.sqrt(HD)
MASKED = -1e30
LOADS_B = 10 + 2 * NP
E, FF = 8, 896
FT = FF // P
FA = 512
TA = FA // P
TOKENS = B * S
N_SLOTS = 2 * TOKENS // P + E - 1
REGION = TOKENS // P
BLOCKS = (E + 1) * REGION
CONSTS = dict(expert=(E,), region_row=(E,), steps=(E, REGION - 1), upto=(E, E), slot=(N_SLOTS,),
              per_expert=(3, E - 1), start=(4, N_SLOTS))
R_STEPS = 11
TABLE_STEPS = 18
A_SCALE = 1.0 / (math.sqrt(64) * math.log(20))
EPS = 1e-5


def const_table(np):
    odd = np.arange(E - 1) % 2
    t = dict(
        expert=np.arange(E), region_row=np.arange(E) * REGION * P,
        steps=np.broadcast_to(np.arange(1, REGION) * P, (E, REGION - 1)),
        upto=np.tril(np.ones((E, E))), slot=np.arange(N_SLOTS),
        per_expert=np.stack([1 - 2 * odd, 48 * odd, 48 * (1 - odd) * (np.arange(E - 1) > 0)]),
        start=np.stack([np.zeros(N_SLOTS), np.full(N_SLOTS, 48), np.full(N_SLOTS, 48), np.arange(N_SLOTS)]))
    flat = np.concatenate([t[k].reshape(-1) for k in CONSTS]).astype(np.float32)
    return np.broadcast_to(flat, (P, flat.size))


def const_at(name):
    at = 0
    for key, shape in CONSTS.items():
        n = math.prod(shape)
        if key == name:
            return at, at + n
        at += n
    return 0, at


RING_H, RING_L, RING_P, RING_O, RING_T, RING_USES = 0, 1, 2, 6, 10, 15


def ring_at(t, use):
    return 1 + GROUPS + RING_USES * t + use


def ahead(p, b, k):
    return p + (b + k) // 2, (b + k) % 2


def pixart_layer(nc, x, ctx_in, k_length, ln_w, ff_ln_w, wq, wk, wv, wo, gate_w, w1, w3, w2,
                 ident, upper, rope, causal, consts, out):
    ctx = ExitStack()
    with ctx:
        def sb(name, shape, dt=F32):
            return ctx.enter_context(nc.sbuf_tensor(name, shape, dt))

        def sem(name):
            return ctx.enter_context(nc.semaphore(name))

        x_rows = x.rearrange("(p b) s d -> (b s) p d", b=2)
        ctx_rows = ctx_in.rearrange("(p b) s d -> (b s) p d", b=2)
        out_rows = out.rearrange("(p b) s d -> (b s) p d", b=2)

        qk_dram = nc.dram_tensor("qk_split", [3, B, HH, J, AD, TERMS, D], F32, kind="Internal").ap()

        xg_dram = nc.dram_tensor("expert_rows", [BLOCKS * P, D], F32, kind="Internal").ap()
        xg_blocks = xg_dram.rearrange("(s p) d -> p s d", p=P)

        x_all = sb("x_all", [P, NP, D])
        idn = sb("idn", [P, P])
        upp = sb("upp", [P, P])
        ones = sb("ones", [P, P])
        zeros = sb("zeros", [P, D])
        wqkv = sb("wqkv", [P, KT, QKV])
        wo_s = sb("wo_s", [P, H, D])
        lnw = sb("lnw", [P, KT])
        ffw = sb("ffw", [P, D])
        gw = sb("gw", [P, KT, E])
        cos_sin = sb("cos_sin", [P, 2, HD])
        mask = sb("mask", [P, S])
        cst = sb("cst", [P, consts.shape[1]])
        mhalf = sb("mhalf", [P, NP])
        w13 = sb("w13", [P, 2, KT, 2, FF])
        w2_s = sb("w2_s", [P, 2, FT, D])
        lg_s = sb("lg_s", [P, E])
        mx = sb("mx", [P, E])
        top2 = sb("top2", [P, 2])
        freed = sb("freed", [P, E])
        ix = sb("ix", [P, E], U32)
        ixf = sb("ixf", [P, 2])
        onehot = sb("onehot", [P, 2, E])
        chosen = sb("chosen", [P, E])
        seen = sb("seen", [P, E])
        row_of = sb("row_of", [P, E])
        own = sb("own", [P, 2, E])
        dest_f = sb("dest_f", [P, 2])
        dest = sb("dest", [P, 2], U32)
        dest_all = sb("dest_all", [P, NP, 2], U32)
        top_all = sb("top_all", [P, NP, 2])
        tot = sb("tot", [P, E])
        over = sb("over", [P, E, REGION - 1])
        n_tiles = sb("n_tiles", [P, E])
        upto_s = sb("upto_s", [P, E, E])
        ends = sb("ends", [P, E])
        ends_i = sb("ends_i", [P, E], I32)
        past = sb("past", [P, N_SLOTS, E - 1])
        weigh = sb("weigh", [P, 4, E - 1])
        pastw = sb("pastw", [P, 4, N_SLOTS, E - 1])
        tab_f = sb("tab_f", [P, 4, N_SLOTS])
        tab = sb("tab", [P, 4, N_SLOTS], I32)
        d21 = sb("d21", [P, NP])
        e21 = sb("e21", [P, NP])
        den = sb("den", [P, NP])
        gates = sb("gates", [P, 2, NP])

        def cview(name, pattern=None, **kw):
            a, b = const_at(name)
            v = cst[:, a:b]
            return v.rearrange(pattern, **kw) if pattern else v

        stage = ctx.enter_context(ExitStack())

        def tmp(name, shape, dt=F32):
            return stage.enter_context(nc.sbuf_tensor(name, shape, dt))

        klen_i = tmp("klen_i", [P, NP], I32)
        klen = tmp("klen", [P, NP])
        klog = tmp("klog", [P, NP])
        rstd_s = tmp("rstd_s", [P, NP])
        st = tmp("st", [P, NP, 6])
        mv = tmp("mv", [P, NP, 2])
        veps = tmp("veps", [P, NP])
        rstd = tmp("rstd", [P, NP])
        v_t = tmp("v_t", [P, 2, B, AH, AD + 1])
        q_b = [tmp(f"q_b{i}", [P, HH, D], F32R) for i in range(2)]
        k_1 = [tmp(f"k_1{i}", [P, HH, J, D], F32R) for i in range(2)]
        k_2 = [tmp(f"k_2{i}", [P, HH, J, D], F32R) for i in range(2)]
        q_m = [tmp(f"q_m{i}", [P, HH, D], F32R) for i in range(2)]
        v_b = [tmp(f"v_b{i}", [P, 2, AH, 32]) for i in range(2)]
        negmax = [tmp(f"negmax{i}", [P, 2, HH, P]) for i in range(2)]
        o_s = tmp("o_s", [P, HH, D])
        rsum = tmp("rsum", [P, HH, 2, J])
        a_out = tmp("a_out", [P, 2, 2, HH, J, AD])
        with ExitStack() as split:
            def early(name, dt=F32):
                return split.enter_context(nc.sbuf_tensor(name, [P, NP, D], dt))

            ctx_all, qn = early("ctx_all"), early("qn")
            q_hi, k_hi, k_lo = (early(n, F32R) for n in ("q_hi", "k_hi", "k_lo"))
            q_lo = qn[:].bitcast(F32R)
        p_t = [tmp(f"p_t{i}", [P, 2, J, HH, D]) for i in range(2)]
        stage.close()

        stage = ctx.enter_context(ExitStack())
        xr_all = tmp("xr_all", [P, NP, D])
        st_b = tmp("st_b", [P, NP, 6])
        mv_b = tmp("mv_b", [P, NP, 2])
        var_b = tmp("var_b", [P, NP])
        rstd_b = tmp("rstd_b", [P, NP])
        ms_b = tmp("ms_b", [P, NP])
        msv_b = tmp("msv_b", [P, NP])
        rms_b = tmp("rms_b", [P, NP])
        sq = tmp("sq", [P, D])
        h_b = tmp("h_b", [P, D])
        h_t = tmp("h_t", [P, KT, P])
        raw = tmp("raw", [P, H + KVH, HD])
        rc = tmp("rc", [P, H + KVH, HD])
        rs = tmp("rs", [P, H + KVH, HD])
        qk_t = tmp("qk_t", [P, H + KVH, P])
        v_s = tmp("v_s", [P, KVH * HD])
        sc = tmp("sc", [P, H, S])
        smax = tmp("smax", [P, H])
        ssum = tmp("ssum", [P, H])
        srec = tmp("srec", [P, H])
        pr = tmp("pr", [P, H, 2, S])
        pr_t = tmp("pr_t", [P, H, P])
        o_t = tmp("o_t", [P, H, P])
        x2 = tmp("x2", [P, D])
        ms2 = tmp("ms2", [P, 1])
        msv2 = tmp("msv2", [P, 1])
        rms2 = tmp("rms2", [P, 1])
        h2_b = tmp("h2_b", [P, D])
        h2_t = tmp("h2_t", [P, KT, P])
        stage.close()

        stage = ctx.enter_context(ExitStack())
        xs = [tmp(f"xs{i}", [P, D]) for i in range(2)]
        xs_t = tmp("xs_t", [P, KT, P])
        sil = tmp("sil", [P, FF])
        g_s = tmp("g_s", [P, FF])
        g_t = tmp("g_t", [P, FT, P])
        y_s = [tmp(f"y_s{i}", [P, D]) for i in range(2)]
        yg = tmp("yg", [P, 2, NP, D])
        mix = tmp("mix", [P, NP, D])

        psum = ctx.enter_context(nc.psum_tensor("psum", [P, 8, 512], F32))
        ps_s1 = [psum[:, 2 * i:2 * i + 2, :].rearrange("p h (j k) -> p h j k", k=D) for i in range(2)]
        ps_s2 = [psum[:, 4 + i, :] for i in range(2)]
        ps_max = psum[:, 6, :]
        ps_t = psum[:, 6, :].rearrange("p (h a j e) -> p h a j e", h=HH, a=2, j=J)
        ps_ot = psum[:, 6, 0:D]
        ps_o = psum[:, 7, :].rearrange("p (h q) -> p h q", h=HH)

        ps_proj = [psum[:, i, :] for i in range(2)]
        ps_ring = [psum[:, i, :] for i in (2, 3, 6)]
        ps_sc = psum[:, 4:6, :].rearrange("p b (h k) -> p (b h) k", k=S)
        ps_wo = psum[:, 7, 0:D]
        ps_lg = psum[:, 7, D:D + E]
        ps_pos = psum[:, 7, D + E:D + 2 * E]
        ps_h = [[psum[:, 2 * part + m, :] for m in range(2)] for part in range(2)]
        ps_gt = [psum[:, 4 + part, :] for part in range(2)]
        ps_xt = psum[:, 6, 0:KT * P]
        ps_y = psum[:, 7, 0:D]

        ld_w, filled, cleared, pr_zero = sem("ld_w"), sem("filled"), sem("cleared"), sem("pr_zero")
        bst_ok, var_ok, rstdb_ok, xr_ok, sq_ok, msv_ok, rms_ok = (sem(n) for n in (
            "bst_ok", "var_ok", "rstdb_ok", "xr_ok", "sq_ok", "msv_ok", "rms_ok"))
        hb_ok, ring_ok, ring_free, proj_ok, proj_free = (sem(n) for n in (
            "hb_ok", "ring_ok", "ring_free", "proj_ok", "proj_free"))
        rope_mul, rope_ok, sc_ok, masked_ok, smax_ok, sub_ok, exps_ok, ssum_ok, srec_ok, pr_ok = (sem(n) for n in (
            "rope_mul", "rope_ok", "sc_ok", "masked_ok", "smax_ok", "sub_ok", "exps_ok", "ssum_ok", "srec_ok", "pr_ok"))
        wo_ok, x2_ok, sum_ok, sq2_ok, msv2_ok, rms2_ok, h2_ok = (sem(n) for n in (
            "wo_ok", "x2_ok", "sum_ok", "sq2_ok", "msv2_ok", "rms2_ok", "h2_ok"))
        lg_ok, pos_ok, routed, sent, total_ok, table_ok, e21_ok = (sem(n) for n in (
            "lg_ok", "pos_ok", "routed", "sent", "total_ok", "table_ok", "e21_ok"))
        ld_e = [sem(f"ld_e{i}") for i in range(2)]
        xt_ok, xst_ok, hid_ok, silu_ok, g_ok, gt_ok, gts_ok, y_ok, ys_ok = (sem(n) for n in (
            "xt_ok", "xst_ok", "hid_ok", "silu_ok", "g_ok", "gt_ok", "gts_ok", "y_ok", "ys_ok"))
        ld_xs = [sem(f"ld_xs{i}") for i in range(2)]
        wr_y = [sem(f"wr_y{i}") for i in range(2)]
        got = [sem(f"got{t}") for t in range(NP)]
        mix_ok, placed, gates_ok, seen_ok = sem("mix_ok"), sem("placed"), sem("gates_ok"), sem("seen_ok")

        ld_x, ld_ctx, ld_c, ld_k = sem("ld_x"), sem("ld_ctx"), sem("ld_c"), sem("ld_k")
        zeroed = sem("zeroed")
        stats, veps_ok, rstd_ok, qn_ok = sem("stats"), sem("veps_ok"), sem("rstd_ok"), sem("qn_ok")
        qhi_ok, qlo_ok, khi_ok, klo_ok = sem("qhi_ok"), sem("qlo_ok"), sem("khi_ok"), sem("klo_ok")
        klen_ok, klog_ok, s_ok = sem("klen_ok"), sem("klog_ok"), sem("s_ok")
        vt_ps, vt_ok = sem("vt_ps"), sem("vt_ok")
        wr_q, wr_k = ([sem(f"{n}{i}") for i in range(2)] for n in ("wr_q", "wr_k"))
        ld_q = [sem(f"ld_q{i}") for i in range(2)]
        ld_k1 = [sem(f"ld_k1{i}") for i in range(2)]
        ld_k2 = [sem(f"ld_k2{i}") for i in range(2)]
        vb_ok, os_ok, t_ok = sem("vb_ok"), sem("os_ok"), sem("t_ok")
        s1_ok, max_ok, maxt_ok, qm_ok = sem("s1_ok"), sem("max_ok"), sem("maxt_ok"), sem("qm_ok")
        s2_ok, exp_ok, pv_ok, rsum_ok, aout_ok = sem("s2_ok"), sem("exp_ok"), sem("pv_ok"), sem("rsum_ok"), sem("aout_ok")
        ot_ok, x1_ok, wr_out = sem("ot_ok"), sem("x1_ok"), sem("wr_out")

        block = ctx.enter_context(nc.Block())

        @block.sync
        def _(sp):
            sp.dma_start(ctx_all[:], ctx_rows).then_inc(ld_ctx, 16)
            sp.dma_start(x_all[:], x_rows).then_inc(ld_x, 16)
            sp.dma_start(idn[:], ident).then_inc(ld_c, 16)
            for b in range(2):
                src = k_length.rearrange("(o p b) -> b o p", o=1, b=2)[b].broadcast_to([S, NP])
                with nc.allow_non_contiguous_dma(reason="16 lengths"):
                    sp.dma_start(klen_i[b * S:(b + 1) * S, :], src).then_inc(ld_k, 16)

            def write_split(w, parts, done):
                for tiles, wrote in ((slice(0, 1), done[0]), (slice(1, NP), done[1])):
                    for t, src in enumerate(parts):
                        for b in range(2):
                            dst = qk_dram[w].rearrange("(p b) h j d t c -> b t (h j d) p c", b=2)[b, t]
                            sp.dma_start(dst[:, tiles, :],
                                         src[b * S:(b + 1) * S, tiles, :].bitcast(F32)).then_inc(wrote, 16)

            sp.wait_ge(khi_ok, 1)
            sp.wait_ge(klo_ok, 1)
            write_split(2, (k_hi, k_hi, k_lo), wr_k)
            sp.wait_ge(qhi_ok, 1)
            sp.wait_ge(qlo_ok, 1)
            write_split(1, (q_hi, q_lo, q_hi), wr_q)
            sp.wait_ge(zeroed, 19)
            sp.wait_ge(wr_k[0], 2 * TERMS * 16)
            sp.wait_ge(wr_q[0], 2 * TERMS * 16)

            def load_q(p, b):
                n = 2 * p + b
                for j in range(J):
                    src = qk_dram[1, bass.ds(n, 1), :, j].rearrange("o h d t c -> (o d t) h c")
                    sp.dma_start(q_b[b][32 * j + 1:32 * j + KR, :, :].bitcast(F32), src).then_inc(ld_q[b], 16)

            def load_k(p, b, dst, done):
                n = 2 * p + b
                for j in range(J):
                    src = qk_dram[2, bass.ds(n, 1), :, j].rearrange("o h d t c -> (o d t) h c")
                    sp.dma_start(dst[b][32 * j + 1:32 * j + KR, :, j, :].bitcast(F32), src).then_inc(done[b], 16)

            for n in range(2):
                load_q(0, n)
                load_k(0, n, k_1, ld_k1)
                load_k(0, n, k_2, ld_k2)
            sp.wait_ge(wr_k[1], 2 * TERMS * 16)
            sp.wait_ge(wr_q[1], 2 * TERMS * 16)
            with sp.Fori(0, NP - 1) as p:
                for b in range(2):
                    n = 2 * p + b
                    sp.wait_ge(s1_ok, 4 * n + 4)
                    sp.wait_ge(zeroed, 19)
                    load_k(p + 1, b, k_1, ld_k1)
                    sp.wait_ge(qm_ok, n + 1)
                    sp.wait_ge(qhi_ok, 1)
                    load_q(p + 1, b)
                    sp.wait_ge(s2_ok, 8 * (n + 1))
                    sp.wait_ge(qlo_ok, 1)
                    load_k(p + 1, b, k_2, ld_k2)

            sp.wait_ge(cleared, 16 * NP)
            sp.wait_ge(sent, 2 * NP * 16)
            sp.wait_ge(table_ok, TABLE_STEPS)

            def slot_block(s):
                return sp.value_load(tab[0:1, 3, s], min_val=0, max_val=BLOCKS - 1)

            def load_rows(i, b, block):
                sp.dma_start(xs[b][:].rearrange("p (o d) -> p o d", o=1),
                             xg_blocks[:, bass.ds(block, 1), :]).then_inc(ld_xs[b], 16)

            def store_rows(i, b, block):
                sp.wait_ge(ys_ok, 2 * i + b + 1)
                if b == 0:
                    sp.wait_ge(cleared, 16 * NP)
                else:
                    sp.wait_ge(zeroed, 19)
                sp.dma_start(xg_blocks[:, bass.ds(block, 1), :],
                             y_s[b][:].rearrange("p (o d) -> p o d", o=1)).then_inc(wr_y[b], 16)

            for b in range(2):
                load_rows(0, b, slot_block(slice(b, b + 1)))
            with sp.Fori(0, (N_SLOTS - 3) // 2) as i:
                for b in range(2):
                    s = 2 * i + b
                    following = slot_block(bass.ds(s + 2, 1))
                    this = slot_block(bass.ds(s, 1))
                    sp.wait_ge(xt_ok, s + 1)
                    load_rows(i + 1, b, following)
                    store_rows(i, b, this)
            for s in range(N_SLOTS - 3, N_SLOTS):
                if s + 2 < N_SLOTS:
                    following = slot_block(slice(s + 2, s + 3))
                    sp.wait_ge(xt_ok, s + 1)
                    load_rows(s // 2 + 1, s % 2, following)
                store_rows(s // 2, s % 2, slot_block(slice(s, s + 1)))
            for t in range(NP):
                sp.wait_ge(mix_ok, 2 * t + 2)
                sp.dma_start(out_rows[:, t, :], mix[:, t, :]).then_inc(wr_out, 16)
            sp.wait_ge(wr_out, NP * 16)

        @block.gpsimd
        def _(pool):
            nc.gpsimd.memset(zeros[:], 0.0).then_inc(filled, 1)
            nc.gpsimd.memset(mhalf[:], -0.5).then_inc(filled, 1)
            nc.gpsimd.memset(ones[:], 1.0).then_inc(filled, 1)
            nc.gpsimd.memset(seen[:], 0.0).then_inc(filled, 1)
            for i in range(2):
                nc.gpsimd.memset(q_b[i][:].bitcast(F32), 0.0).then_inc(zeroed, 1)
                nc.gpsimd.memset(k_1[i][:].bitcast(F32), 0.0).then_inc(zeroed, 1)
                nc.gpsimd.memset(k_2[i][:].bitcast(F32), 0.0).then_inc(zeroed, 1)
                nc.gpsimd.memset(negmax[i][:], 0.0).then_inc(zeroed, 1)
                nc.gpsimd.memset(v_b[i][:], 0.0).then_inc(zeroed, 1)
            nc.gpsimd.memset(v_t[:], 1.0).then_inc(zeroed, 1)
            pool.wait_ge(zeroed, 11)
            for i in range(2):
                for j in range(J):
                    nc.gpsimd.memset(k_2[i][32 * j:32 * j + 1, :, j, :].bitcast(F32), 1.0).then_inc(zeroed, 1)
            pool.wait_ge(zeroed, 19)
            pool.wait_ge(veps_ok, 1)
            nc.gpsimd.tensor_tensor(rstd[:], veps[:], mhalf[:], ALU.pow).then_inc(rstd_ok, 1)
            pool.wait_ge(vt_ok, 8)

            def take_values(p, b, first=False):
                n = 2 * p + b
                if not first:
                    pool.wait_ge(pv_ok, n - 1)
                pool.wait_ge(zeroed, 19)
                nc.gpsimd.tensor_copy(v_b[b][:, :, :, 0:AD + 1],
                                      v_t[:, :, bass.ds(n, 1), :, :].rearrange("p a o h d -> p a (o h) d")).then_inc(vb_ok, 1)

            take_values(0, 0, True)
            take_values(0, 1, True)
            pool.wait_ge(filled, 1)
            def load_part(p):
                heads = bass.ds(p * (H // NP) * HD, H // NP * HD)
                pool.dma_start(wqkv[:, :, heads], wq.rearrange("(k p) n -> p k n", p=P)[:, :, heads]).then_inc(ld_w, 16)
                heads = bass.ds(p * (H // NP), H // NP)
                pool.dma_start(wo_s[:, heads, :], wo.rearrange("(h p) n -> p h n", p=P)[:, heads, :]).then_inc(ld_w, 16)
                pool.dma_start(xg_blocks[:, bass.ds(p * (BLOCKS // NP), BLOCKS // NP), :],
                              zeros[:].rearrange("p (o d) -> p o d", o=1).broadcast_to([P, BLOCKS // NP, D])).then_inc(cleared, 16)

            for dst, src in (
                    (wqkv[:, :, H * HD:(H + KVH) * HD], wk.rearrange("(k p) n -> p k n", p=P)),
                    (wqkv[:, :, (H + KVH) * HD:], wv.rearrange("(k p) n -> p k n", p=P)),
                    (gw[:], gate_w.rearrange("(k p) n -> p k n", p=P)),
                    (ffw[:], ff_ln_w.rearrange("(o d) -> o d", o=1).broadcast_to([P, D])),
                    (cos_sin[:], rope), (mask[:], causal), (upp[:], upper), (cst[:], consts)):
                pool.dma_start(dst, src).then_inc(ld_w, 16)
            with nc.allow_non_contiguous_dma(reason="256 weights, one per partition and tile"):
                for k in range(KT):
                    pool.dma_start(lnw[:, k:k + 1], ln_w.rearrange("(k p o) -> k p o", p=P, o=1)[k]).then_inc(ld_w, 16)

            with pool.Fori(1, NP) as p:
                for b in range(2):
                    take_values(p, b)
                load_part(p - 1)
            load_part(NP - 1)

            def load_expert(e):
                i = e % 2
                for m, w in enumerate((w1, w3)):
                    pool.dma_start(w13[:, i, :, m, :], w[e].rearrange("(k p) f -> p k f", p=P)).then_inc(ld_e[i], 16)
                pool.dma_start(w2_s[:, i, :, :], w2[e].rearrange("(f p) d -> p f d", p=P)).then_inc(ld_e[i], 16)

            load_expert(0)
            load_expert(1)

            pool.wait_ge(ot_ok, NP)
            nc.gpsimd.memset(pr[:], 0.0).then_inc(pr_zero, 1)
            pool.wait_ge(filled, 4)
            pool.wait_ge(var_ok, 1)
            nc.gpsimd.tensor_tensor(rstd_b[:], var_b[:], mhalf[:], ALU.pow).then_inc(rstdb_ok, 1)
            pool.wait_ge(msv_ok, 1)
            nc.gpsimd.tensor_tensor(rms_b[:], msv_b[:], mhalf[:], ALU.pow).then_inc(rms_ok, 1)

            def add_rope(t, c):
                pool.wait_ge(rope_mul, 3 * (GROUPS * t + c + 1))
                heads = slice(4 * c, 4 * c + 4)
                nc.gpsimd.tensor_tensor(rc[:, heads, :], rc[:, heads, :], rs[:, heads, :], ALU.add).then_inc(rope_ok, 1)

            def send(t):
                pool.wait_ge(cleared, 16 * NP)
                pool.wait_ge(routed, R_STEPS * (t + 1))
                nc.gpsimd.tensor_tensor(seen[:], seen[:], chosen[:], ALU.add).then_inc(seen_ok, 1)
                for i in range(2):
                    nc.gpsimd.indirect_dma_start(
                        xg_dram, bass.IndirectOffsetOnAxis(dest[:, i:i + 1], 0), h2_b[:], None).then_inc(sent, 16)

            def inverse_root(t):
                pool.wait_ge(msv2_ok, t + 1)
                nc.gpsimd.tensor_tensor(rms2[:], msv2[:], mhalf[:, 0:1], ALU.pow).then_inc(rms2_ok, 1)

            def step(t):
                fixed = isinstance(t, int)
                if not fixed or t > 0:
                    inverse_root(t - 1)
                if not fixed or t < NP - 1:
                    for c in range(GROUPS):
                        add_rope(t + 1, c)
                if not fixed or t > 0:
                    send(t - 1)

            for c in range(GROUPS):
                add_rope(0, c)
            step(0)
            with pool.Fori(1, NP - 1) as t:
                step(t)
            step(NP - 1)
            inverse_root(NP - 1)
            send(NP - 1)

            pool.wait_ge(table_ok, TABLE_STEPS)
            for e in range(2, E):
                done = pool.value_load(ends_i[0:1, e - 2:e - 1], min_val=1, max_val=N_SLOTS)
                pool.wait_ge(y_ok, done)
                nc.gpsimd.tensor_tensor(freed[:, e:e + 1], ones[:, 0:1], ones[:, 0:1], ALU.mult)
                load_expert(e)
            for b in range(2):
                pool.wait_ge(wr_y[b], (N_SLOTS + 1 - b) // 2 * 16)
            for t in range(NP):
                for i in range(2):
                    nc.gpsimd.indirect_dma_start(
                        yg[:, i, t, :], None, xg_dram, bass.IndirectOffsetOnAxis(dest_all[:, t, i:i + 1], 0)).then_inc(got[t], 16)

        @block.scalar
        def _(act):
            act.wait_ge(ld_ctx, 16)
            nc.scalar.activation(k_hi[:], ctx_all[:], ACT.Copy).then_inc(khi_ok, 1)
            act.wait_ge(klen_ok, 1)
            nc.scalar.activation(klog[:], klen[:], ACT.Ln).then_inc(klog_ok, 1)
            for g in range(4):
                act.wait_ge(vt_ps, g + 1)
                act.wait_ge(zeroed, 19)
                for half in range(2):
                    nc.scalar.copy(
                        v_t[:, half, 4 * g:4 * g + 4, :, 0:AD].rearrange("p b h d -> p (b h) d"),
                        psum[:, g, 256 * half:256 * half + 256].rearrange("p (n d) -> p n d", d=AD)).then_inc(vt_ok, 1)
            act.wait_ge(qn_ok, NP)
            nc.scalar.activation(q_hi[:], qn[:], ACT.Copy).then_inc(qhi_ok, 1)
            def exps(p, b, first):
                n = 2 * p + b
                if not first:
                    act.wait_ge(pv_ok, n - 1)
                for u in range(8):
                    khalf, j = u // 4, u % 4
                    act.wait_ge(s2_ok, 8 * n + u + 1)
                    nc.scalar.activation(
                        p_t[b][:, khalf, j, :, :],
                        ps_s2[u % 2].rearrange("p (h q) -> p h q", h=HH), ACT.Exp).then_inc(exp_ok, 1)

            def take_out(p, b):
                n = 2 * p + b
                act.wait_ge(pv_ok, n + 1)
                if not isinstance(n, int) or n > 0:
                    act.wait_ge(t_ok, n)
                nc.scalar.copy(o_s[:], ps_o).then_inc(os_ok, 1)

            act.wait_ge(wr_k[1], 2 * TERMS * 16)
            act.wait_ge(wr_q[1], 2 * TERMS * 16)
            exps(0, 0, True)
            exps(0, 1, True)
            with act.Fori(1, NP) as p:
                for b in range(2):
                    take_out(p - 1, b)
                    exps(p, b, False)
            take_out(NP - 1, 0)
            take_out(NP - 1, 1)

            for t in range(NP):
                act.wait_ge(xr_ok, t + 1)
                if t:
                    act.wait_ge(sq_ok, t)
                nc.scalar.activation(sq[:], xr_all[:, t, :], ACT.Square, accum_out=ms_b[:, t:t + 1]).then_inc(sq_ok, 1)
            act.wait_ge(ld_w, LOADS_B * 16)

            def take_h(t, at, last_inc=1):
                act.wait_ge(ring_ok, at + 1)
                for k in range(KT):
                    i = nc.scalar.activation(h_t[:, k, :], ps_ring[0][:, P * k:P * k + P], ACT.Copy,
                                             scale=lnw[:, k:k + 1])
                i.then_inc(ring_free, last_inc)

            def take_proj(t, c):
                act.wait_ge(proj_ok, (GROUPS + 1) * t + c + 1)
                nc.scalar.copy(raw[:, 4 * c:4 * c + 4, :].rearrange("p h d -> p (h d)"),
                               ps_proj[c % 2]).then_inc(proj_free, 1)

            def take_v(t):
                act.wait_ge(proj_ok, (GROUPS + 1) * (t + 1))
                nc.scalar.copy(v_s[:], ps_proj[GROUPS % 2]).then_inc(proj_free, 1)

            def take_heads(dst, i, at, bank):
                act.wait_ge(ring_ok, at + 1)
                nc.scalar.copy(dst[:, 4 * i:4 * i + 4, :].rearrange("p h n -> p (h n)"),
                               ps_ring[bank]).then_inc(ring_free, 1)

            def take_h2(at, bank, inc=1):
                act.wait_ge(ring_ok, at + inc)
                nc.scalar.copy(h2_t[:].rearrange("p k n -> p (k n)"), ps_ring[bank][:, 0:D]).then_inc(ring_free, inc)

            def step(t):
                fixed = isinstance(t, int)
                first, last = fixed and t == 0, fixed and t == NP - 1
                if not last:
                    take_h(t + 1, ring_at(t, RING_H), 2 if first else 1)
                if not first:
                    square(t - 1)
                if not last:
                    for c in range(2):
                        take_proj(t + 1, c)
                act.wait_ge(sub_ok, t + 1)
                nc.scalar.activation(sc[:], sc[:], ACT.Exp).then_inc(exps_ok, 1)
                if not last:
                    for c in range(2, 4):
                        take_proj(t + 1, c)
                if not first:
                    take_h2(ring_at(t, RING_L) - (1 if last else 0), RING_L % 3, 2 if last else 1)
                if not last:
                    take_proj(t + 1, 4)
                for i in range(4):
                    take_heads(pr_t, i, ring_at(t, RING_P + i), (RING_P + i) % 3)
                for i in range(4):
                    take_heads(o_t, i, ring_at(t, RING_O + i), (RING_O + i) % 3)
                if not last:
                    take_v(t + 1)
                    for i in range(GROUPS):
                        take_heads(qk_t, i, ring_at(t, RING_T + i), (RING_T + i) % 3)

            def square(t):
                act.wait_ge(x2_ok, t + 1)
                nc.scalar.activation(sq[:], x2[:], ACT.Square, accum_out=ms2[:]).then_inc(sq2_ok, 1)

            take_h(0, 0)
            for c in range(GROUPS):
                take_proj(0, c)
            take_v(0)
            for i in range(GROUPS):
                take_heads(qk_t, i, 1 + i, (1 + i) % 3)
            step(0)
            with act.Fori(1, NP - 1) as t:
                step(t)
            step(NP - 1)
            square(NP - 1)
            take_h2(ring_at(NP - 1, RING_T), RING_T % 3)

            act.wait_ge(table_ok, 1)
            nc.scalar.activation(e21[:], d21[:], ACT.Exp).then_inc(e21_ok, 1)

            def take_xt(s):
                act.wait_ge(xt_ok, s + 1)
                nc.scalar.copy(xs_t[:].rearrange("p k n -> p (k n)"), ps_xt).then_inc(xst_ok, 1)

            def silu(s, part):
                cols = slice(0, FA) if part == 0 else slice(FA, FF)
                act.wait_ge(hid_ok, 4 * s + 2 * part + 1)
                nc.scalar.activation(sil[:, cols], ps_h[part][0][:, 0:cols.stop - cols.start], ACT.Silu).then_inc(silu_ok, 1)

            def take_gt(s, part):
                tiles = slice(0, TA) if part == 0 else slice(TA, FT)
                act.wait_ge(gt_ok, 2 * s + part + 1)
                nc.scalar.copy(g_t[:, tiles, :].rearrange("p f n -> p (f n)"),
                               ps_gt[part][:, 0:P * (tiles.stop - tiles.start)]).then_inc(gts_ok, 1)

            def slot(s, last=False):
                silu(s, 1)
                take_gt(s, 0)
                if not last:
                    take_xt(s + 1)
                take_gt(s, 1)
                if not last:
                    silu(s + 1, 0)

            take_xt(0)
            silu(0, 0)
            with act.Fori(0, N_SLOTS - 1) as s:
                slot(s)
            slot(N_SLOTS - 1, last=True)

        @block.vector
        def _(dve):
            dve.wait_ge(ld_x, 16)
            for p in range(NP):
                nc.vector.bn_stats(st[:, p, :], x_all[:, p, :]).then_inc(stats, 1)
            dve.wait_ge(stats, NP)
            for p in range(NP):
                nc.vector.bn_aggr(mv[:, p, :], st[:, p, :]).then_inc(stats, 1)
            dve.wait_ge(stats, 2 * NP)
            nc.vector.tensor_scalar(veps[:], mv[:, :, 1], EPS, None, ALU.add).then_inc(veps_ok, 1)
            dve.wait_ge(khi_ok, 1)
            nc.vector.tensor_tensor(k_lo[:], ctx_all[:], k_hi[:].bitcast(F32), ALU.subtract).then_inc(klo_ok, 1)
            dve.wait_ge(ld_k, 32)
            nc.vector.tensor_copy(klen[:], klen_i[:]).then_inc(klen_ok, 1)
            dve.wait_ge(rstd_ok, 1)
            dve.wait_ge(klog_ok, 1)
            nc.vector.scalar_tensor_tensor(out=rstd_s[:], in0=klog[:], scalar=A_SCALE, in1=rstd[:],
                                           op0=ALU.mult, op1=ALU.mult).then_inc(s_ok, 1)
            dve.wait_ge(s_ok, 1)
            for p in range(NP):
                nc.vector.tensor_scalar(qn[:, p, :], x_all[:, p, :], mv[:, p, 0:1], rstd_s[:, p:p + 1],
                                        ALU.subtract, ALU.mult).then_inc(qn_ok, 1)
            dve.wait_ge(qhi_ok, 1)
            dve.wait_ge(qn_ok, NP)
            nc.vector.tensor_tensor(q_lo[:], qn[:], q_hi[:].bitcast(F32), ALU.subtract).then_inc(qlo_ok, 1)

            def maxima(p, b, c, first):
                n = 2 * p + b
                if c == 0 and not first:
                    dve.wait_ge(maxt_ok, n - 1)
                dve.wait_ge(s1_ok, 4 * n + c + 1)
                nc.vector.tensor_reduce(negmax[b][:, c // 2, :, 64 * (c % 2):64 * (c % 2) + 64:32], ps_s1[c % 2], AX.X, ALU.max,
                                        negate=True).then_inc(max_ok, 1)

            def with_max(p, b):
                n = 2 * p + b
                dve.wait_ge(maxt_ok, n + 1)
                dve.wait_ge(ld_q[b], 16 * J * (p + 1))
                nc.vector.tensor_tensor(q_m[b][:], q_b[b][:].bitcast(F32),
                                        ps_max.rearrange("p (h q) -> p h q", h=HH), ALU.add).then_inc(qm_ok, 1)

            def normalise(p, b, first=False):
                n = 2 * p + b
                dve.wait_ge(t_ok, n + 1)
                nc.vector.reciprocal(rsum[:], ps_t[:, :, :, :, AD]).then_inc(rsum_ok, 1)
                dve.wait_ge(rsum_ok, n + 1)
                if b == 0 and not first:
                    dve.wait_ge(ot_ok, p)
                for hh in range(HH):
                    nc.vector.tensor_tensor(
                        a_out[:, :, b, hh], ps_t[:, hh, :, :, 0:AD],
                        rsum[:, hh].rearrange("p a (j o) -> p a j o", o=1).broadcast_to([P, 2, J, AD]),
                        ALU.mult).then_inc(aout_ok, 1)

            def add_x(p):
                dve.wait_ge(ot_ok, p + 1)
                nc.vector.tensor_tensor(x_all[:, bass.ds(p, 1), :].rearrange("p o d -> p (o d)"),
                                        x_all[:, bass.ds(p, 1), :].rearrange("p o d -> p (o d)"),
                                        ps_ot, ALU.add).then_inc(x1_ok, 1)

            def step(p, b):
                n = 2 * p + b
                fixed = isinstance(n, int)
                if not fixed or n < B:
                    with_max(p, b)
                for c in range(4):
                    if not fixed or n + 1 < B:
                        maxima(*ahead(p, b, 1), c, fixed and n + 1 < 2)
                    if c == 1 and (not fixed or n >= 2):
                        normalise(p - 1, b, first=fixed and n == 2)
                if b == 1 and (not fixed or n >= 3):
                    add_x(p - 1)

            dve.wait_ge(zeroed, 19)
            for c in range(4):
                maxima(0, 0, c, True)
            for n in range(4):
                step(n // 2, n % 2)
            with dve.Fori(2, NP - 1) as p:
                for b in range(2):
                    step(p, b)
            for n in range(B - 2, B + 2):
                step(n // 2, n % 2)

            dve.wait_ge(x1_ok, NP)
            for t in range(NP):
                nc.vector.bn_stats(st_b[:, t, :], x_all[:, t, :]).then_inc(bst_ok, 1)
            dve.wait_ge(bst_ok, NP)
            for t in range(NP):
                nc.vector.bn_aggr(mv_b[:, t, :], st_b[:, t, :]).then_inc(bst_ok, 1)
            dve.wait_ge(bst_ok, 2 * NP)
            nc.vector.tensor_scalar(var_b[:], mv_b[:, :, 1], EPS, None, ALU.add).then_inc(var_ok, 1)
            dve.wait_ge(rstdb_ok, 1)
            for t in range(NP):
                nc.vector.tensor_scalar(xr_all[:, t, :], x_all[:, t, :], mv_b[:, t, 0:1], rstd_b[:, t:t + 1],
                                        ALU.subtract, ALU.mult).then_inc(xr_ok, 1)
            dve.wait_ge(sq_ok, NP)
            nc.vector.tensor_scalar(msv_b[:], ms_b[:], 1.0 / D, EPS, ALU.mult, ALU.add).then_inc(msv_ok, 1)
            dve.wait_ge(rms_ok, 1)
            dve.wait_ge(xr_ok, NP)
            dve.wait_ge(ld_w, LOADS_B * 16)
            dve.wait_ge(pr_zero, 1)

            def rows(a, t):
                return a[:, bass.ds(t, 1), :].rearrange("p o d -> p (o d)")

            def norm_rows(t):
                if not isinstance(t, int) or t > 0:
                    dve.wait_ge(proj_ok, (GROUPS + 1) * (t - 1) + 1)
                    dve.wait_ge(zeroed, 19)
                nc.vector.tensor_tensor(h_b[:], rows(xr_all, t), rms_b[:, bass.ds(t, 1)].broadcast_to([P, D]),
                                        ALU.mult).then_inc(hb_ok, 1)

            def rope_products(t, c):
                dve.wait_ge(proj_free, (GROUPS + 1) * t + c + 1)
                heads = slice(4 * c, 4 * c + 4)
                tables = cos_sin[:].rearrange("p (t o) d -> p t o d", o=1)
                nc.vector.tensor_tensor(rc[:, heads, :], raw[:, heads, :],
                                        tables[:, 0].broadcast_to([P, 4, HD]), ALU.mult).then_inc(rope_mul, 1)
                for i in range(2):
                    nc.vector.tensor_tensor(rs[:, heads, i::2], raw[:, heads, 1 - i::2],
                                            tables[:, 1, :, i::2].broadcast_to([P, 4, HD // 2]),
                                            ALU.mult).then_inc(rope_mul, 1)

            def mask_scores(t):
                dve.wait_ge(sc_ok, t + 1)
                nc.vector.scalar_tensor_tensor(
                    out=sc[:], in0=ps_sc, scalar=B_SCALE,
                    in1=mask[:].rearrange("p (o k) -> p o k", o=1).broadcast_to([P, H, S]),
                    op0=ALU.mult, op1=ALU.add).then_inc(masked_ok, 1)
                dve.wait_ge(masked_ok, t + 1)
                nc.vector.tensor_reduce(smax[:], sc[:], AX.X, ALU.max).then_inc(smax_ok, 1)
                dve.wait_ge(smax_ok, t + 1)
                nc.vector.tensor_tensor(sc[:], sc[:], smax[:].rearrange("p (h o) -> p h o", o=1).broadcast_to([P, H, S]),
                                        ALU.subtract).then_inc(sub_ok, 1)

            def probabilities(t):
                dve.wait_ge(exps_ok, t + 1)
                nc.vector.tensor_reduce(ssum[:], sc[:], AX.X, ALU.add).then_inc(ssum_ok, 1)
                dve.wait_ge(ssum_ok, t + 1)
                nc.vector.reciprocal(srec[:], ssum[:]).then_inc(srec_ok, 1)
                dve.wait_ge(srec_ok, t + 1)
                for b in range(2):
                    rws = slice(b * S, (b + 1) * S)
                    nc.vector.tensor_tensor(
                        pr[rws, :, b, :], sc[rws], srec[rws].rearrange("p (h o) -> p h o", o=1).broadcast_to([S, H, S]),
                        ALU.mult).then_inc(pr_ok, 1)

            def choose(t):
                def after(i):
                    dve.wait_ge(routed, R_STEPS * t + i)

                dve.wait_ge(lg_ok, t + 1)
                nc.vector.tensor_copy(lg_s[:], ps_lg).then_inc(routed, 1)
                nc.vector.max(mx[:], ps_lg).then_inc(routed, 1)
                after(2)
                nc.vector.tensor_copy(top2[:], mx[:, 0:2]).then_inc(routed, 1)
                nc.vector.max_index(ix[:], mx[:], lg_s[:]).then_inc(routed, 1)
                after(4)
                nc.vector.tensor_copy(ixf[:], ix[:, 0:2]).then_inc(routed, 1)
                dve.wait_ge(zeroed, 19)
                nc.vector.tensor_copy(rows(top_all, t), top2[:]).then_inc(placed, 1)
                after(5)
                nc.vector.tensor_tensor(
                    onehot[:], ixf[:].rearrange("p (i o) -> p i o", o=1).broadcast_to([P, 2, E]),
                    cview("expert", "p (o e) -> p o e", o=1).broadcast_to([P, 2, E]), ALU.is_equal).then_inc(routed, 1)
                after(6)
                if not isinstance(t, int) or t > 0:
                    dve.wait_ge(seen_ok, t)
                nc.vector.tensor_tensor(chosen[:], onehot[:, 0, :], onehot[:, 1, :], ALU.add).then_inc(routed, 1)

            def place(t):
                def after(i):
                    dve.wait_ge(routed, R_STEPS * t + i)

                dve.wait_ge(pos_ok, t + 1)
                nc.vector.tensor_tensor(row_of[:], ps_pos, cview("region_row"), ALU.add).then_inc(routed, 1)
                after(8)
                nc.vector.tensor_tensor(own[:], onehot[:], row_of[:].rearrange("p (o e) -> p o e", o=1).broadcast_to([P, 2, E]),
                                        ALU.mult).then_inc(routed, 1)
                after(9)
                nc.vector.tensor_reduce(dest_f[:], own[:], AX.X, ALU.add).then_inc(routed, 1)
                after(10)
                if not isinstance(t, int) or t > 0:
                    dve.wait_ge(sent, 32 * t)
                nc.vector.tensor_copy(dest[:], dest_f[:]).then_inc(routed, 1)
                dve.wait_ge(zeroed, 19)
                nc.vector.tensor_copy(rows(dest_all, t), dest_f[:]).then_inc(placed, 1)

            def add_residual(t):
                dve.wait_ge(wo_ok, t + 1)
                dve.wait_ge(zeroed, 19)
                nc.vector.tensor_tensor(x2[:], ps_wo, rows(xr_all, t), ALU.add).then_inc(x2_ok, 1)
                dve.wait_ge(x2_ok, t + 1)
                dve.wait_ge(zeroed, 19)
                nc.vector.tensor_tensor(rows(x_all, t), rows(x_all, t), x2[:], ALU.add).then_inc(sum_ok, 1)

            def second_variance(t):
                dve.wait_ge(sq2_ok, t + 1)
                nc.vector.tensor_scalar(msv2[:], ms2[:], 1.0 / D, EPS, ALU.mult, ALU.add).then_inc(msv2_ok, 1)

            def second_norm(t):
                if not isinstance(t, int) or t > 0:
                    dve.wait_ge(sent, 32 * t)
                dve.wait_ge(rms2_ok, t + 1)
                nc.vector.scalar_tensor_tensor(out=h2_b[:], in0=x2[:], scalar=rms2[:, 0:1], in1=ffw[:],
                                               op0=ALU.mult, op1=ALU.mult).then_inc(h2_ok, 1)

            def step(t):
                fixed = isinstance(t, int)
                first, last = fixed and t == 0, fixed and t == NP - 1
                if not first:
                    second_variance(t - 1)
                mask_scores(t)
                if not first:
                    second_norm(t - 1)
                if not last:
                    rope_products(t + 1, 0)
                    rope_products(t + 1, 1)
                probabilities(t)
                if not last:
                    rope_products(t + 1, 2)
                    rope_products(t + 1, 3)
                if not first:
                    choose(t - 1)
                if not last:
                    rope_products(t + 1, 4)
                if not first:
                    place(t - 1)
                if not fixed or t + 2 < NP:
                    norm_rows(t + 2)
                add_residual(t)

            norm_rows(0)
            norm_rows(1)
            for c in range(GROUPS):
                rope_products(0, c)
            step(0)
            step(1)
            with dve.Fori(2, NP - 2) as t:
                step(t)
            step(NP - 2)
            step(NP - 1)
            second_variance(NP - 1)
            second_norm(NP - 1)
            choose(NP - 1)
            place(NP - 1)

            def after(i):
                dve.wait_ge(table_ok, i)

            dve.wait_ge(routed, R_STEPS * NP)
            nc.vector.tensor_tensor(d21[:], top_all[:, :, 1], top_all[:, :, 0], ALU.subtract).then_inc(table_ok, 1)
            dve.wait_ge(total_ok, 1)
            nc.vector.tensor_copy(tot[:], ps_pos).then_inc(table_ok, 1)
            after(2)
            nc.vector.tensor_tensor(over[:], tot[:].rearrange("p (e o) -> p e o", o=1).broadcast_to([P, E, REGION - 1]),
                                    cview("steps", "p (e j) -> p e j", e=E), ALU.is_gt).then_inc(table_ok, 1)
            after(3)
            nc.vector.tensor_reduce(n_tiles[:], over[:], AX.X, ALU.add).then_inc(table_ok, 1)
            after(4)
            nc.vector.tensor_scalar(n_tiles[:], n_tiles[:], 1.0, None, ALU.add).then_inc(table_ok, 1)
            nc.vector.tensor_copy(weigh[:, 0:3, :], cview("per_expert", "p (r e) -> p r e", r=3)).then_inc(table_ok, 1)
            after(5)
            nc.vector.tensor_tensor(upto_s[:], n_tiles[:].rearrange("p (o e) -> p o e", o=1).broadcast_to([P, E, E]),
                                    cview("upto", "p (a e) -> p a e", a=E), ALU.mult).then_inc(table_ok, 1)
            nc.vector.tensor_scalar(weigh[:, 3, :], n_tiles[:, 0:E - 1], -1.0, float(REGION),
                                    ALU.mult, ALU.add).then_inc(table_ok, 1)
            after(7)
            nc.vector.tensor_reduce(ends[:], upto_s[:], AX.X, ALU.add).then_inc(table_ok, 1)
            after(9)
            nc.vector.tensor_copy(ends_i[:], ends[:]).then_inc(table_ok, 1)
            nc.vector.tensor_tensor(
                past[:], cview("slot", "p (s o) -> p s o", o=1).broadcast_to([P, N_SLOTS, E - 1]),
                ends[:, 0:E - 1].rearrange("p (o e) -> p o e", o=1).broadcast_to([P, N_SLOTS, E - 1]),
                ALU.is_ge).then_inc(table_ok, 1)
            after(11)
            for r in range(4):
                nc.vector.tensor_tensor(pastw[:, r], past[:], weigh[:, r:r + 1, :].broadcast_to([P, N_SLOTS, E - 1]),
                                        ALU.mult).then_inc(table_ok, 1)
            after(15)
            nc.vector.tensor_reduce(tab_f[:], pastw[:], AX.X, ALU.add).then_inc(table_ok, 1)
            after(16)
            nc.vector.tensor_tensor(tab_f[:], tab_f[:], cview("start", "p (r s) -> p r s", r=4), ALU.add).then_inc(table_ok, 1)
            after(17)
            nc.vector.tensor_copy(tab[:], tab_f[:]).then_inc(table_ok, 1)
            dve.wait_ge(e21_ok, 1)
            nc.vector.tensor_scalar(den[:], e21[:], 1.0, None, ALU.add).then_inc(gates_ok, 1)
            dve.wait_ge(gates_ok, 1)
            nc.vector.reciprocal(gates[:, 0, :], den[:]).then_inc(gates_ok, 1)
            dve.wait_ge(gates_ok, 2)
            nc.vector.tensor_tensor(gates[:, 1, :], e21[:], gates[:, 0, :], ALU.mult).then_inc(gates_ok, 1)

            def products(s, part):
                cols = slice(0, FA) if part == 0 else slice(FA, FF)
                dve.wait_ge(silu_ok, 2 * s + part + 1)
                dve.wait_ge(hid_ok, 4 * s + 2 * part + 2)
                nc.vector.tensor_tensor(g_s[:, cols], sil[:, cols], ps_h[part][1][:, 0:cols.stop - cols.start],
                                        ALU.mult).then_inc(g_ok, 1)

            def take_y(i, b):
                dve.wait_ge(y_ok, 2 * i + b + 1)
                if not isinstance(i, int) or i > 0:
                    dve.wait_ge(wr_y[b], 16 * i)
                nc.vector.tensor_copy(y_s[b][:], ps_y).then_inc(ys_ok, 1)

            def slot(i, b):
                products(2 * i + b, 1)
                if not isinstance(i, int) or 2 * i + b + 1 < N_SLOTS:
                    products(2 * i + b + 1, 0)
                take_y(i, b)

            products(0, 0)
            slot(0, 0)
            slot(0, 1)
            with dve.Fori(1, N_SLOTS // 2) as i:
                for b in range(2):
                    slot(i, b)
            slot(N_SLOTS // 2, 0)

            dve.wait_ge(sum_ok, NP)
            dve.wait_ge(gates_ok, 3)
            for t in range(NP):
                dve.wait_ge(got[t], 32)
                nc.vector.scalar_tensor_tensor(out=mix[:, t, :], in0=yg[:, 0, t, :], scalar=gates[:, 0, t:t + 1],
                                               in1=x_all[:, t, :], op0=ALU.mult, op1=ALU.add).then_inc(mix_ok, 1)
                dve.wait_ge(mix_ok, 2 * t + 1)
                nc.vector.scalar_tensor_tensor(out=mix[:, t, :], in0=yg[:, 1, t, :], scalar=gates[:, 1, t:t + 1],
                                               in1=mix[:, t, :], op0=ALU.mult, op1=ALU.add).then_inc(mix_ok, 1)

        @block.tensor
        def _(pe):
            pe.wait_ge(ld_c, 16)
            pe.wait_ge(ld_ctx, 16)
            for g in range(4):
                for half in range(2):
                    for pp in range(2):
                        i = nc.tensor.transpose(psum[:, g, 256 * half + 128 * pp:256 * half + 128 * pp + 128],
                                                ctx_all[:, 2 * g + pp, 128 * half:128 * half + 128], idn[:])
                i.then_inc(vt_ps, 1)

            def scores_q(p, b, c, first=False):
                n = 2 * p + b
                qhalf, jp = c // 2, c % 2
                if c == 0:
                    pe.wait_ge(ld_k1[b], 16 * J * (p + 1))
                    pe.wait_ge(ld_q[b], 16 * J * (p + 1))
                if not first or c >= 2:
                    pe.wait_ge(max_ok, 4 * n + c - 1)
                for hh in range(HH):
                    i = nc.tensor.matmul(ps_s1[c % 2][:, hh], q_b[b][:, hh, 128 * qhalf:128 * qhalf + 128],
                                         k_1[b][:, hh, 2 * jp:2 * jp + 2, :], start=True, stop=True)
                i.then_inc(s1_ok, 1)

            def max_rows(p, b, first=False):
                n = 2 * p + b
                pe.wait_ge(max_ok, 4 * n + 4)
                if not first:
                    pe.wait_ge(qm_ok, n)
                    if b == 0:
                        pe.wait_ge(x1_ok, p - 1)
                    else:
                        pe.wait_ge(aout_ok, 2 * n - 4)
                for hh in range(HH):
                    for qhalf in range(2):
                        at = D * hh + 128 * qhalf
                        i = nc.tensor.transpose(ps_max[:, at:at + 128], negmax[b][:, qhalf, hh, :], idn[:])
                i.then_inc(maxt_ok, 1)

            def scores_k(p, b, u, first=False):
                n = 2 * p + b
                khalf, j = u // 4, u % 4
                if u == 0:
                    pe.wait_ge(qm_ok, n + 1)
                    pe.wait_ge(ld_k2[b], 16 * J * (p + 1))
                if not first or u >= 2:
                    pe.wait_ge(exp_ok, 8 * n + u - 1)
                for hh in range(HH):
                    i = nc.tensor.matmul(ps_s2[u % 2][:, D * hh:D * (hh + 1)],
                                         k_2[b][:, hh, j, 128 * khalf:128 * khalf + 128],
                                         q_m[b][:, hh, :], start=True, stop=True)
                i.then_inc(s2_ok, 1)

            def values(p, b, c):
                n = 2 * p + b
                if c == 0:
                    pe.wait_ge(exp_ok, 8 * n + 8)
                    pe.wait_ge(vb_ok, n + 1)
                    if not isinstance(n, int) or n > 0:
                        pe.wait_ge(os_ok, n)
                hh, khalf = c // 2, c % 2
                for j in range(J):
                    i = nc.tensor.matmul(ps_o[32 * j:32 * j + 32, hh, :], v_b[b][:, khalf, J * hh + j, :],
                                         p_t[b][:, khalf, j, hh, :], start=khalf == 0, stop=khalf == 1)
                if c == 3:
                    i.then_inc(pv_ok, 1)

            def columns(p, b):
                n = 2 * p + b
                pe.wait_ge(os_ok, n + 1)
                if isinstance(n, int) and n >= B - 2:
                    pe.wait_ge(x1_ok, p)
                    pe.wait_ge(aout_ok, 2 * n)
                for hh in range(HH):
                    for a in range(2):
                        i = nc.tensor.transpose(ps_t[:, hh, a].rearrange("p j e -> p (j e)"),
                                                o_s[:, hh, 128 * a:128 * a + 128], idn[:])
                i.then_inc(t_ok, 1)

            def back_rows(p):
                pe.wait_ge(aout_ok, 4 * p + 4)
                for a in range(2):
                    i = nc.tensor.transpose(ps_ot[:, 128 * a:128 * a + 128],
                                            a_out[:, a].rearrange("p b h j d -> p (b h j d)"), idn[:])
                i.then_inc(ot_ok, 1)

            def step(p, b):
                n = 2 * p + b
                fixed = isinstance(n, int)
                if not fixed or n < B:
                    max_rows(p, b, fixed and n < 4)
                for c in range(4):
                    if not fixed or n + 1 < B:
                        scores_q(*ahead(p, b, 1), c)
                    if not fixed or 1 <= n <= B:
                        values(*ahead(p, b, -1), c)
                    if not fixed or n < B:
                        scores_k(p, b, 2 * c, fixed and n == 0)
                        scores_k(p, b, 2 * c + 1, fixed and n == 0)
                    if c == 0 and (not fixed or n >= 2):
                        columns(p - 1, b)
                if b == 1 and (not fixed or n >= 3):
                    back_rows(p - 1)

            pe.wait_ge(vt_ok, 8)
            pe.wait_ge(zeroed, 19)
            for c in range(4):
                scores_q(0, 0, c, first=True)
            for n in range(4):
                step(n // 2, n % 2)
            with pe.Fori(2, NP - 1) as p:
                for b in range(2):
                    step(p, b)
            for n in range(B - 2, B + 2):
                step(n // 2, n % 2)

            def use_ring(at):
                if not isinstance(at, int) or at >= 3:
                    pe.wait_ge(ring_free, at - 2)

            def rows_t(t, at, inc=1):
                pe.wait_ge(hb_ok, t + 1)
                use_ring(at)
                for k in range(KT):
                    i = nc.tensor.transpose(ps_ring[0][:, P * k:P * k + P], h_b[:, P * k:P * k + P], idn[:])
                i.then_inc(ring_ok, inc)

            def project(t, c, at):
                n = (GROUPS + 1) * t + c
                if c == 0:
                    pe.wait_ge(ring_free, at)
                if not isinstance(n, int) or n >= 2:
                    pe.wait_ge(proj_free, n - 1)
                for k in range(KT):
                    i = nc.tensor.matmul(ps_proj[c % 2], h_t[:, k, :], wqkv[:, k, 512 * c:512 * c + 512],
                                         start=k == 0, stop=k == KT - 1)
                i.then_inc(proj_ok, 1)

            def heads_t(t, c, at, bank):
                pe.wait_ge(rope_ok, GROUPS * t + c + 1)
                use_ring(at)
                for j in range(4):
                    i = nc.tensor.transpose(ps_ring[bank][:, P * j:P * j + P], rc[:, 4 * c + j, :], idn[:])
                i.then_inc(ring_ok, 1)

            def scores(t):
                pe.wait_ge(ring_free, ring_at(t, 0))
                for h in range(H):
                    for b in range(2):
                        cols = slice(b * S, (b + 1) * S)
                        i = nc.tensor.matmul(ps_sc[cols, h, :], qk_t[:, h, cols], qk_t[:, H + h // (H // KVH), cols],
                                             start=True, stop=True)
                i.then_inc(sc_ok, 1)

            def h2_rows(t, at, bank, inc=1):
                pe.wait_ge(h2_ok, t + 1)
                use_ring(at)
                for k in range(KT):
                    i = nc.tensor.transpose(ps_ring[bank][:, P * k:P * k + P], h2_b[:, P * k:P * k + P], idn[:])
                i.then_inc(ring_ok, inc)

            def logits(at):
                pe.wait_ge(ring_free, at + 1)
                for k in range(KT):
                    i = nc.tensor.matmul(ps_lg, h2_t[:, k, :], gw[:, k, :], start=k == 0, stop=k == KT - 1)
                i.then_inc(lg_ok, 1)

            def positions(t):
                pe.wait_ge(routed, R_STEPS * t + 7)
                nc.tensor.matmul(ps_pos, upp[:], chosen[:], start=True, stop=False)
                if not isinstance(t, int) or t > 0:
                    pe.wait_ge(seen_ok, t)
                nc.tensor.matmul(ps_pos, ones[:], seen[:], start=False, stop=True).then_inc(pos_ok, 1)

            def attend(t):
                pe.wait_ge(pr_ok, 2 * t + 2)
                for i in range(4):
                    use_ring(ring_at(t, RING_P + i))
                    for j in range(4):
                        m = nc.tensor.transpose(ps_ring[(RING_P + i) % 3][:, P * j:P * j + P],
                                                pr[:, 4 * i + j].rearrange("p b k -> p (b k)"), idn[:])
                    m.then_inc(ring_ok, 1)
                pe.wait_ge(proj_free, (GROUPS + 1) * (t + 1))
                for i in range(4):
                    use_ring(ring_at(t, RING_O + i))
                    nc.tensor.matmul(ps_ring[(RING_O + i) % 3], v_s[:, HD * i:HD * i + HD],
                                     pr_t[:, 4 * i:4 * i + 4, :].rearrange("p h n -> p (h n)"),
                                     start=True, stop=True).then_inc(ring_ok, 1)

            def project_out(t):
                pe.wait_ge(ring_free, ring_at(t, RING_O + 4))
                if not isinstance(t, int) or t > 0:
                    pe.wait_ge(routed, R_STEPS * t)
                for h in range(H):
                    i = nc.tensor.matmul(ps_wo, o_t[:, h, :], wo_s[:, h, :], start=h == 0, stop=h == H - 1)
                i.then_inc(wo_ok, 1)

            def step(t):
                fixed = isinstance(t, int)
                first, last = fixed and t == 0, fixed and t == NP - 1
                if not last:
                    rows_t(t + 1, ring_at(t, RING_H), 2 if first else 1)
                scores(t)
                if not last:
                    for c in range(4):
                        project(t + 1, c, ring_at(t, RING_H) + 1)
                if not first:
                    h2_rows(t - 1, ring_at(t, RING_L), RING_L % 3, 2 if last else 1)
                if not last:
                    project(t + 1, 4, None)
                if not first:
                    logits(ring_at(t, RING_L))
                attend(t)
                if not first:
                    positions(t - 1)
                if not last:
                    project(t + 1, GROUPS, None)
                    for c in range(GROUPS):
                        heads_t(t + 1, c, ring_at(t, RING_T + c), (RING_T + c) % 3)
                project_out(t)

            pe.wait_ge(ld_w, LOADS_B * 16)
            pe.wait_ge(filled, 4)
            rows_t(0, 0)
            for c in range(GROUPS + 1):
                project(0, c, 1)
            for c in range(GROUPS):
                heads_t(0, c, 1 + c, (1 + c) % 3)
            step(0)
            with pe.Fori(1, NP - 1) as t:
                step(t)
            step(NP - 1)
            h2_rows(NP - 1, ring_at(NP - 1, RING_T), RING_T % 3)
            logits(ring_at(NP - 1, RING_T))
            positions(NP - 1)
            pe.wait_ge(seen_ok, NP)
            nc.tensor.matmul(ps_pos, ones[:], seen[:], start=True, stop=True).then_inc(total_ok, 1)

            def slot_value(r, s, most):
                return pe.value_load(tab[0:1, r, s], min_val=0, max_val=most)

            def x_t(i, b):
                pe.wait_ge(ld_xs[b], 16 * (i + 1))
                for k in range(KT):
                    m = nc.tensor.transpose(ps_xt[:, P * k:P * k + P], xs[b][:, P * k:P * k + P], idn[:])
                m.then_inc(xt_ok, 1)

            def hidden(s, part, buf, ms=(0, 1)):
                n = FA if part == 0 else FF - FA
                for m in ms:
                    for k in range(KT):
                        i = nc.tensor.matmul(ps_h[part][m][:, 0:n], xs_t[:, k, :],
                                             w13[:, bass.ds(buf, 1), k, m, FA * part:FA * part + n].rearrange("p o f -> p (o f)"),
                                             start=k == 0, stop=k == KT - 1)
                    i.then_inc(hid_ok, 1)

            def slot_values(at):
                return [slot_value(0, at, 1)] + [slot_value(1 + i, at, 48 * E // 2) for i in range(2)]

            def hidden_a(s, buf, due):
                for i in range(2):
                    pe.wait_ge(ld_e[i], due[i])
                pe.wait_ge(xst_ok, s + 1)
                hidden(s, 0, buf)

            def g_transposed(s, part):
                pe.wait_ge(g_ok, 2 * s + part + 1)
                tiles = range(0, TA) if part == 0 else range(TA, FT)
                for f in tiles:
                    at = P * (f - tiles[0])
                    i = nc.tensor.transpose(ps_gt[part][:, at:at + P], g_s[:, P * f:P * f + P], idn[:])
                i.then_inc(gt_ok, 1)

            def outputs(s, part, buf, first=False):
                pe.wait_ge(gts_ok, 2 * s + part + 1)
                if part == 0 and not first:
                    pe.wait_ge(ys_ok, s)
                pe.wait_ge(zeroed, 19)
                for f in (range(0, TA) if part == 0 else range(TA, FT)):
                    i = nc.tensor.matmul(ps_y, g_t[:, f, :],
                                         w2_s[:, bass.ds(buf, 1), f, :].rearrange("p o d -> p (o d)"),
                                         start=f == 0, stop=f == FT - 1)
                if part == 1:
                    i.then_inc(y_ok, 1)

            def slot(i, b):
                s = 2 * i + b
                fixed = isinstance(s, int)
                last = fixed and s == N_SLOTS - 1
                at, following = (slice(s, s + 1), slice(s + 1, s + 2)) if fixed else (bass.ds(s, 1), bass.ds(s + 1, 1))
                buf = slot_value(0, at, 1)
                if not last:
                    next_buf, *due = slot_values(following)
                hidden(s, 1, buf, (0,))
                g_transposed(s, 0)
                hidden(s, 1, buf, (1,))
                if not last:
                    x_t(*ahead(i, b, 1))
                outputs(s, 0, buf, fixed and s == 0)
                g_transposed(s, 1)
                if not last:
                    hidden_a(s + 1, next_buf, due)
                outputs(s, 1, buf)

            pe.wait_ge(table_ok, TABLE_STEPS)
            x_t(0, 0)
            buf, *due = slot_values(slice(0, 1))
            hidden_a(0, buf, due)
            slot(0, 0)
            slot(0, 1)
            with pe.Fori(1, N_SLOTS // 2) as i:
                for b in range(2):
                    slot(i, b)
            slot(N_SLOTS // 2, 0)


def kernel(**inputs):
    import numpy as np
    import concourse.bacc as bacc
    from concourse.bass_utils import run_bass_kernel_spmd

    nc = bacc.Bacc("TRN2", target_bir_lowering=False, num_devices=1)
    arrays = {}

    def given(name, a):
        a = np.ascontiguousarray(a)
        arrays[f"in_{name}"] = a
        return nc.dram_tensor(f"in_{name}", a.shape, mybir.dt.from_np(a.dtype), kind="ExternalInput").ap()

    out = nc.dram_tensor("out_0", (B, S, D), F32, kind="ExternalOutput").ap()
    angle = np.arange(S, dtype=np.float32)[:, None] * (
        np.float32(1000000.0) ** (-np.arange(0, HD, 2, dtype=np.float32) / np.float32(HD)))[None, :]
    cos, sin = np.cos(angle), np.sin(angle)
    rope = np.stack([np.stack([cos, cos], -1).reshape(S, HD), np.stack([-sin, sin], -1).reshape(S, HD)], 1)
    rope = np.concatenate([rope, rope], 0).astype(np.float32)
    causal = np.where(np.arange(S)[:, None] >= np.arange(S)[None, :], 0.0, MASKED).astype(np.float32)
    weights = [given(k, inputs["L0_ffn_" + k]) for k in
               ("ln_w", "ff_ln_w", "wq", "wk", "wv", "wo", "gate_w", "w1", "w3", "w2")]
    pixart_layer(nc, given("x", inputs["x"]), given("ctx", inputs["ctx_2048"]),
                 given("k_length", inputs["itok_B_779_1933"]), *weights,
                 given("ident", np.eye(P, dtype=np.float32)),
                 given("upper", np.triu(np.ones((P, P), np.float32), 1)),
                 given("rope", rope), given("causal", np.concatenate([causal, causal], 0)),
                 given("consts", const_table(np)), out)
    r = run_bass_kernel_spmd(nc, [arrays], core_ids=[0])
    return r.results[0]["out_0"]
```

```python
from contextlib import ExitStack
import math

import concourse.bass as bass
from concourse import mybir

F32 = mybir.dt.float32
F32R = mybir.dt.float32r
I32 = mybir.dt.int32
ALU = mybir.AluOpType
ACT = mybir.ActivationFunctionType
AX = mybir.AxisListType
U32 = mybir.dt.uint32

P = 128
B, S, D = 16, 64, 256
NP = B // 2
AH, AD = 8, 8
J, HH = 4, 2
TERMS = 3
KR = 1 + TERMS * AD
H, KVH, HD = 16, 4, 128
KT = D // P
GROUPS = H // KVH + 1
QKV = (H + 2 * KVH) * HD
B_SCALE = 1.0 / math.sqrt(HD)
MASKED = -1e30
LOADS_B = 8 + NP
E, FF = 8, 896
FT = FF // P
FA = 512
TA = FA // P
TOKENS = B * S
N_SLOTS = 2 * TOKENS // P + E - 1
REGION = TOKENS // P
BLOCKS = (E + 1) * REGION
CONSTS = dict(expert=(E,), region_row=(E,), steps=(E, REGION - 1), upto=(E, E), slot=(N_SLOTS,),
              per_expert=(3, E - 1), start=(4, N_SLOTS), store=(2, N_SLOTS))
R_STEPS = 11
EARLY = NP - 2
TABLE_STEPS = 18
ZEROED = 11 + 2 * J
A_SCALE = 1.0 / (math.sqrt(64) * math.log(20))
EPS = 1e-5


def const_table(np):
    odd = np.arange(E - 1) % 2
    t = dict(
        expert=np.arange(E), region_row=np.arange(E) * REGION * P,
        steps=np.broadcast_to(np.arange(1, REGION) * P, (E, REGION - 1)),
        upto=np.tril(np.ones((E, E))), slot=np.arange(N_SLOTS),
        per_expert=np.stack([1 - 2 * odd, 48 * odd, 48 * (1 - odd) * (np.arange(E - 1) > 0)]),
        start=np.stack([np.zeros(N_SLOTS), np.full(N_SLOTS, 48), np.full(N_SLOTS, 48), np.arange(N_SLOTS)]),
        store=16 * np.stack([np.arange(N_SLOTS) % 2 == b for b in range(2)]))
    flat = np.concatenate([t[k].reshape(-1) for k in CONSTS]).astype(np.float32)
    return np.broadcast_to(flat, (P, flat.size))


def const_at(name):
    at = 0
    for key, shape in CONSTS.items():
        n = math.prod(shape)
        if key == name:
            return at, at + n
        at += n
    return 0, at


RING_H, RING_L, RING_P, RING_O, RING_T, RING_USES = 0, 1, 2, 6, 10, 15


def ring_at(t, use):
    return 1 + GROUPS + RING_USES * t + use


def ahead(p, b, k):
    return p + (b + k) // 2, (b + k) % 2


def pixart_layer(nc, x, ctx_in, k_length, ln_w, ff_ln_w, wq, wk, wv, wo, gate_w, w1, w3, w2,
                 ident, upper, rope, causal, consts, out):
    ctx = ExitStack()
    with ctx:
        def sb(name, shape, dt=F32):
            return ctx.enter_context(nc.sbuf_tensor(name, shape, dt))

        def sem(name):
            return ctx.enter_context(nc.semaphore(name))

        x_rows = x.rearrange("(p b) s d -> (b s) p d", b=2)
        ctx_rows = ctx_in.rearrange("(p b) s d -> (b s) p d", b=2)
        out_rows = out.rearrange("(p b) s d -> (b s) p d", b=2)

        qk_dram = nc.dram_tensor("qk_split", [3, B, HH, J, AD, TERMS, D], F32, kind="Internal").ap()

        xg_dram = nc.dram_tensor("expert_rows", [BLOCKS * P, D], F32, kind="Internal").ap()
        xg_blocks = xg_dram.rearrange("(s p) d -> p s d", p=P)

        x_all = sb("x_all", [P, NP, D])
        idn = sb("idn", [P, P])
        upp = sb("upp", [P, P])
        ones = sb("ones", [P, P])
        zeros = sb("zeros", [P, D])
        wqkv_lo = sb("wqkv_lo", [P, KT, QKV], F32R)
        wo_s = sb("wo_s", [P, H, D])
        lnw = sb("lnw", [P, KT])
        ffw = sb("ffw", [P, D])
        gw = sb("gw", [P, KT, E])
        cos_sin = sb("cos_sin", [P, 2, HD])
        mask = sb("mask", [P, S])
        cst = sb("cst", [P, consts.shape[1]])
        mhalf = sb("mhalf", [P, NP])
        xr_all = sb("xr_all", [P, NP, D])
        st_b = sb("st_b", [P, NP, 6])
        mv_b = sb("mv_b", [P, NP, 2])
        var_b = sb("var_b", [P, NP])
        rstd_b = sb("rstd_b", [P, NP])
        ms_b = sb("ms_b", [P, NP])
        msv_b = sb("msv_b", [P, NP])
        rms_b = sb("rms_b", [P, NP])
        sq = sb("sq", [P, D])
        lg_s = sb("lg_s", [P, E])
        mx = sb("mx", [P, E])
        top2 = sb("top2", [P, 2])
        freed = sb("freed", [P, E])
        ix = sb("ix", [P, E], U32)
        ixf = sb("ixf", [P, 2])
        onehot = sb("onehot", [P, 2, E])
        chosen = sb("chosen", [P, E])
        seen = sb("seen", [P, E])
        row_of = sb("row_of", [P, E])
        own = sb("own", [P, 2, E])
        dest_f = sb("dest_f", [P, 2])
        dest = sb("dest", [P, 2], U32)
        dest_all = sb("dest_all", [P, NP, 2], U32)
        top_all = sb("top_all", [P, NP, 2])
        tot = sb("tot", [P, E])
        over = sb("over", [P, E, REGION - 1])
        n_tiles = sb("n_tiles", [P, E])
        upto_s = sb("upto_s", [P, E, E])
        ends = sb("ends", [P, E])
        ends_i = sb("ends_i", [P, E], I32)
        past = sb("past", [P, N_SLOTS, E - 1])
        weigh = sb("weigh", [P, 4, E - 1])
        pastw = sb("pastw", [P, 4, N_SLOTS, E - 1])
        tab_f = sb("tab_f", [P, 4, N_SLOTS])
        tab = sb("tab", [P, 4, N_SLOTS], I32)
        used = sb("used", [P, 2, N_SLOTS])
        stores_f = sb("stores_f", [P, 2])
        stores = sb("stores", [P, 2], I32)
        d21 = sb("d21", [P, NP])
        e21 = sb("e21", [P, NP])
        den = sb("den", [P, NP])
        gates = sb("gates", [P, 2, NP])

        def cview(name, pattern=None, **kw):
            a, b = const_at(name)
            v = cst[:, a:b]
            return v.rearrange(pattern, **kw) if pattern else v

        stage = ctx.enter_context(ExitStack())

        def tmp(name, shape, dt=F32):
            return stage.enter_context(nc.sbuf_tensor(name, shape, dt))

        ctx_all, qn = tmp("ctx_all", [P, NP, D]), tmp("qn", [P, NP, D])
        q_hi, k_hi, k_lo = (tmp(n, [P, NP, D], F32R) for n in ("q_hi", "k_hi", "k_lo"))
        q_lo = qn[:].bitcast(F32R)
        p_t = [tmp(f"p_t{i}", [P, 2, J, HH, D]) for i in range(2)]
        klen_i = tmp("klen_i", [P, NP], I32)
        klen = tmp("klen", [P, NP])
        klog = tmp("klog", [P, NP])
        rstd_s = tmp("rstd_s", [P, NP])
        st = tmp("st", [P, NP, 6])
        mv = tmp("mv", [P, NP, 2])
        veps = tmp("veps", [P, NP])
        rstd = tmp("rstd", [P, NP])
        v_t = tmp("v_t", [P, 2, B, AH, AD + 1])
        q_b = [tmp(f"q_b{i}", [P, HH, D], F32R) for i in range(2)]
        k_1 = [tmp(f"k_1{i}", [P, HH, J, D], F32R) for i in range(2)]
        k_2 = [tmp(f"k_2{i}", [P, HH, J, D], F32R) for i in range(2)]
        q_m = [tmp(f"q_m{i}", [P, HH, D], F32R) for i in range(2)]
        v_b = [tmp(f"v_b{i}", [P, 2, AH, 32]) for i in range(2)]
        negmax = [tmp(f"negmax{i}", [P, 2, HH, P]) for i in range(2)]
        o_s = tmp("o_s", [P, HH, D])
        rsum = tmp("rsum", [P, HH, 2, J])
        a_out = tmp("a_out", [P, 2, 2, HH, J, AD])
        stage.close()

        wqkv_hi = sb("wqkv_hi", [P, KT, QKV], F32R)
        sc = sb("sc", [P, H, S])
        o_t = sb("o_t", [P, H, P])
        raw_q = sc[:].rearrange("p h s -> p (h s)")[:, 0:KT * HD * H // NP].rearrange("p (k n) -> p k n", k=KT)
        raw_kv = o_t[:].rearrange("p h n -> p (h n)").rearrange("p (k n) -> p k n", k=KT)
        w13 = sb("w13", [P, 2, KT, 2, FF])
        w2_s = sb("w2_s", [P, 2, FT, D])

        stage = ctx.enter_context(ExitStack())
        h_b = tmp("h_b", [P, D])
        h_hi = tmp("h_hi", [P, KT, P], F32R)
        h_lo = tmp("h_lo", [P, KT, P], F32R)
        raw = tmp("raw", [P, H + KVH, HD])
        rc = tmp("rc", [P, H + KVH, HD])
        rs = tmp("rs", [P, 2, 4, HD])
        qk_t = tmp("qk_t", [P, H + KVH, P])
        v_s = tmp("v_s", [P, KVH * HD])
        smax = tmp("smax", [P, H])
        ssum = tmp("ssum", [P, H])
        srec = tmp("srec", [P, H])
        pr = tmp("pr", [P, H, 2, S])
        pr_t = tmp("pr_t", [P, H, P])
        x2 = tmp("x2", [P, D])
        ms2 = tmp("ms2", [P, 1])
        msv2 = tmp("msv2", [P, 1])
        rms2 = tmp("rms2", [P, 1])
        h2_b = tmp("h2_b", [P, D])
        h2_t = tmp("h2_t", [P, KT, P])
        stage.close()

        stage = ctx.enter_context(ExitStack())
        xs = [tmp(f"xs{i}", [P, D]) for i in range(2)]
        xs_t = tmp("xs_t", [P, KT, P])
        sil = tmp("sil", [P, FF])
        g_s = tmp("g_s", [P, FF])
        g_t = tmp("g_t", [P, FT, P])
        y_s = [tmp(f"y_s{i}", [P, D]) for i in range(2)]
        yg = tmp("yg", [P, 2, NP, D])
        mix = tmp("mix", [P, NP, D])

        psum = ctx.enter_context(nc.psum_tensor("psum", [P, 8, 512], F32))
        ps_s1 = [psum[:, 2 * i:2 * i + 2, :].rearrange("p h (j k) -> p h j k", k=D) for i in range(2)]
        ps_s2 = [psum[:, 4 + i, :] for i in range(2)]
        ps_max = psum[:, 6, :]
        ps_t = psum[:, 6, :].rearrange("p (h a j e) -> p h a j e", h=HH, a=2, j=J)
        ps_ot = psum[:, 6, 0:D]
        ps_o = psum[:, 7, :].rearrange("p (h q) -> p h q", h=HH)

        ps_proj = [psum[:, i, :] for i in range(2)]
        ps_ring = [psum[:, i, :] for i in (2, 3, 6)]
        ps_sc = psum[:, 4:6, :].rearrange("p b (h k) -> p (b h) k", k=S)
        ps_wo = psum[:, 7, 0:D]
        ps_lg = psum[:, 7, D:D + E]
        ps_pos = psum[:, 7, D + E:D + 2 * E]
        ps_h = [[psum[:, 2 * part + m, :] for m in range(2)] for part in range(2)]
        ps_gt = [psum[:, 4 + part, :] for part in range(2)]
        ps_xt = psum[:, 6, 0:KT * P]
        ps_y = psum[:, 7, 0:D]

        ld_w, filled, cleared, pr_zero = sem("ld_w"), sem("filled"), sem("cleared"), sem("pr_zero")
        bst_ok, var_ok, rstdb_ok, xr_ok, sq_ok, msv_ok, rms_ok = (sem(n) for n in (
            "bst_ok", "var_ok", "rstdb_ok", "xr_ok", "sq_ok", "msv_ok", "rms_ok"))
        hb_ok, ring_ok, ring_free, proj_ok, proj_free = (sem(n) for n in (
            "hb_ok", "ring_ok", "ring_free", "proj_ok", "proj_free"))
        rope_mul, rope_ok, sc_ok, masked_ok, smax_ok, sub_ok, exps_ok, ssum_ok, srec_ok, pr_ok = (sem(n) for n in (
            "rope_mul", "rope_ok", "sc_ok", "masked_ok", "smax_ok", "sub_ok", "exps_ok", "ssum_ok", "srec_ok", "pr_ok"))
        wo_ok, x2_ok, sum_ok, sq2_ok, msv2_ok, rms2_ok, h2_ok = (sem(n) for n in (
            "wo_ok", "x2_ok", "sum_ok", "sq2_ok", "msv2_ok", "rms2_ok", "h2_ok"))
        lg_ok, pos_ok, routed, sent, total_ok, table_ok, e21_ok = (sem(n) for n in (
            "lg_ok", "pos_ok", "routed", "sent", "total_ok", "table_ok", "e21_ok"))
        ld_e = [sem(f"ld_e{i}") for i in range(2)]
        xt_ok, xst_ok, hid_ok, silu_ok, g_ok, gt_ok, gts_ok, y_ok, ys_ok = (sem(n) for n in (
            "xt_ok", "xst_ok", "hid_ok", "silu_ok", "g_ok", "gt_ok", "gts_ok", "y_ok", "ys_ok"))
        ld_xs = [sem(f"ld_xs{i}") for i in range(2)]
        wr_y = [sem(f"wr_y{i}") for i in range(2)]
        got = [sem(f"got{t}") for t in range(NP)]
        ld_wq, whi_ok, wlo_ok, hlo_ok = (sem(n) for n in ("ld_wq", "whi_ok", "wlo_ok", "hlo_ok"))
        ld_kv, whi_kv, wlo_kv, stores_ok = (sem(n) for n in ("ld_kv", "whi_kv", "wlo_kv", "stores_ok"))
        mix_ok, placed, gates_ok, seen_ok = sem("mix_ok"), sem("placed"), sem("gates_ok"), sem("seen_ok")

        ld_x, ld_ctx, ld_c, ld_k = sem("ld_x"), sem("ld_ctx"), sem("ld_c"), sem("ld_k")
        zeroed = sem("zeroed")
        stats, veps_ok, rstd_ok, qn_ok = sem("stats"), sem("veps_ok"), sem("rstd_ok"), sem("qn_ok")
        qhi_ok, qlo_ok, khi_ok, klo_ok = sem("qhi_ok"), sem("qlo_ok"), sem("khi_ok"), sem("klo_ok")
        klen_ok, klog_ok, s_ok = sem("klen_ok"), sem("klog_ok"), sem("s_ok")
        vt_ps, vt_ok = sem("vt_ps"), sem("vt_ok")
        wr_q, wr_k = ([sem(f"{n}{i}") for i in range(2)] for n in ("wr_q", "wr_k"))
        ld_q = [sem(f"ld_q{i}") for i in range(2)]
        ld_k1 = [sem(f"ld_k1{i}") for i in range(2)]
        ld_k2 = [sem(f"ld_k2{i}") for i in range(2)]
        vb_ok, os_ok, t_ok = sem("vb_ok"), sem("os_ok"), sem("t_ok")
        s1_ok, max_ok, maxt_ok, qm_ok = sem("s1_ok"), sem("max_ok"), sem("maxt_ok"), sem("qm_ok")
        s2_ok, exp_ok, pv_ok, rsum_ok, aout_ok = sem("s2_ok"), sem("exp_ok"), sem("pv_ok"), sem("rsum_ok"), sem("aout_ok")
        ot_ok, x1_ok, wr_out = sem("ot_ok"), sem("x1_ok"), sem("wr_out")

        def write_term(queue, w, t, src, tiles, done):
            for b in range(2):
                dst = qk_dram[w].rearrange("(p b) h j d t c -> b t (h j d) p c", b=2)[b, t]
                queue.dma_start(dst[:, tiles, :], src[b * S:(b + 1) * S, tiles, :].bitcast(F32)).then_inc(done, 16)

        block = ctx.enter_context(nc.Block())

        @block.sync
        def _(sp):
            sp.dma_start(x_all[:], x_rows).then_inc(ld_x, 16)
            sp.dma_start(ctx_all[:], ctx_rows).then_inc(ld_ctx, 16)
            for b in range(2):
                src = k_length.rearrange("(o p b) -> b o p", o=1, b=2)[b].broadcast_to([S, NP])
                with nc.allow_non_contiguous_dma(reason="16 lengths"):
                    sp.dma_start(klen_i[b * S:(b + 1) * S, :], src).then_inc(ld_k, 16)

            sp.dma_start(idn[:], ident).then_inc(ld_c, 16)
            first = slice(0, 2)
            sp.wait_ge(khi_ok, 1)
            write_term(sp, 2, 0, k_hi, first, wr_k[0])
            write_term(sp, 2, 1, k_hi, first, wr_k[0])
            sp.wait_ge(qhi_ok, 1)
            write_term(sp, 1, 0, q_hi, first, wr_q[0])
            write_term(sp, 1, 2, q_hi, first, wr_q[0])
            sp.wait_ge(klo_ok, 1)
            write_term(sp, 2, 2, k_lo, first, wr_k[0])
            sp.wait_ge(qlo_ok, 1)
            write_term(sp, 1, 1, q_lo, first, wr_q[0])
            sp.wait_ge(zeroed, ZEROED)
            sp.wait_ge(wr_k[0], 2 * TERMS * 16)
            sp.wait_ge(wr_q[0], 2 * TERMS * 16)

            def load_q(p, b):
                n = 2 * p + b
                for j in range(J):
                    src = qk_dram[1, bass.ds(n, 1), :, j].rearrange("o h d t c -> (o d t) h c")
                    sp.dma_start(q_b[b][32 * j + 1:32 * j + KR, :, :].bitcast(F32), src).then_inc(ld_q[b], 16)

            def load_k(p, b, dst, done):
                n = 2 * p + b
                for j in range(J):
                    src = qk_dram[2, bass.ds(n, 1), :, j].rearrange("o h d t c -> (o d t) h c")
                    sp.dma_start(dst[b][32 * j + 1:32 * j + KR, :, j, :].bitcast(F32), src).then_inc(done[b], 16)

            for n in range(2):
                load_q(0, n)
                load_k(0, n, k_1, ld_k1)
                load_k(0, n, k_2, ld_k2)

            def load_tile(p):
                for b in range(2):
                    n = 2 * p + b
                    sp.wait_ge(s1_ok, 4 * n + 4)
                    sp.wait_ge(zeroed, ZEROED)
                    load_k(p + 1, b, k_1, ld_k1)
                    sp.wait_ge(qm_ok, n + 1)
                    sp.wait_ge(qhi_ok, 1)
                    load_q(p + 1, b)
                    sp.wait_ge(s2_ok, 8 * (n + 1))
                    sp.wait_ge(qlo_ok, 1)
                    load_k(p + 1, b, k_2, ld_k2)

            load_tile(0)
            sp.wait_ge(wr_k[1], 2 * TERMS * 16)
            sp.wait_ge(wr_q[1], 2 * TERMS * 16)
            with sp.Fori(1, NP - 1) as p:
                load_tile(p)

            sp.wait_ge(cleared, 16 * NP)
            sp.wait_ge(sent, 2 * NP * 16)

            def slot_block(s):
                return sp.value_load(tab[0:1, 3, s], min_val=0, max_val=BLOCKS - 1)

            def load_rows(i, b, block):
                sp.dma_start(xs[b][:].rearrange("p (o d) -> p o d", o=1),
                             xg_blocks[:, bass.ds(block, 1), :]).then_inc(ld_xs[b], 16)

            def store_rows(i, b, block):
                sp.wait_ge(ys_ok, 2 * i + b + 1)
                if b == 0:
                    sp.wait_ge(cleared, 16 * NP)
                else:
                    sp.wait_ge(zeroed, ZEROED)
                sp.dma_start(xg_blocks[:, bass.ds(block, 1), :],
                             y_s[b][:].rearrange("p (o d) -> p o d", o=1)).then_inc(wr_y[b], 16)

            load_rows(0, 0, 0)
            sp.wait_ge(table_ok, TABLE_STEPS)
            load_rows(0, 1, slot_block(slice(1, 2)))
            with sp.Fori(0, (N_SLOTS - 3) // 2) as i:
                for b in range(2):
                    s = 2 * i + b
                    following = slot_block(bass.ds(s + 2, 1))
                    this = slot_block(bass.ds(s, 1))
                    sp.wait_ge(xt_ok, s + 1)
                    load_rows(i + 1, b, following)
                    store_rows(i, b, this)
            for s in range(N_SLOTS - 3, N_SLOTS):
                if s + 2 < N_SLOTS:
                    following = slot_block(slice(s + 2, s + 3))
                    sp.wait_ge(xt_ok, s + 1)
                    load_rows(s // 2 + 1, s % 2, following)
                store_rows(s // 2, s % 2, slot_block(slice(s, s + 1)))
            for t in range(NP):
                sp.wait_ge(mix_ok, 2 * t + 2)
                sp.dma_start(out_rows[:, t, :], mix[:, t, :]).then_inc(wr_out, 16)
            sp.wait_ge(wr_out, NP * 16)
            for b in range(2):
                sp.wait_ge(wr_y[b], (N_SLOTS + 1 - b) // 2 * 16)

        @block.gpsimd
        def _(pool):
            nc.gpsimd.memset(zeros[:], 0.0).then_inc(filled, 1)
            nc.gpsimd.memset(mhalf[:], -0.5).then_inc(filled, 1)
            nc.gpsimd.memset(ones[:], 1.0).then_inc(filled, 1)
            nc.gpsimd.memset(seen[:], 0.0).then_inc(filled, 1)
            for i in range(2):
                nc.gpsimd.memset(q_b[i][:].bitcast(F32), 0.0).then_inc(zeroed, 1)
                nc.gpsimd.memset(k_1[i][:].bitcast(F32), 0.0).then_inc(zeroed, 1)
            nc.gpsimd.memset(k_2[0][:].bitcast(F32), 0.0).then_inc(zeroed, 1)
            pool.wait_ge(veps_ok, 1)
            pool.wait_ge(filled, 4)
            nc.gpsimd.tensor_tensor(rstd[:], veps[:], mhalf[:], ALU.pow).then_inc(rstd_ok, 1)
            nc.gpsimd.memset(v_t[:], 1.0).then_inc(zeroed, 1)
            nc.gpsimd.memset(k_2[1][:].bitcast(F32), 0.0).then_inc(zeroed, 1)
            for i in range(2):
                nc.gpsimd.memset(negmax[i][:], 0.0).then_inc(zeroed, 1)
                nc.gpsimd.memset(v_b[i][:], 0.0).then_inc(zeroed, 1)
            pool.wait_ge(zeroed, 11)
            for i in range(2):
                for j in range(J):
                    nc.gpsimd.memset(k_2[i][32 * j:32 * j + 1, :, j, :].bitcast(F32), 1.0).then_inc(zeroed, 1)
            pool.wait_ge(zeroed, ZEROED)
            pool.wait_ge(vt_ok, 8)

            def take_values(p, b, first=False):
                n = 2 * p + b
                if not first:
                    pool.wait_ge(pv_ok, n - 1)
                pool.wait_ge(zeroed, ZEROED)
                nc.gpsimd.tensor_copy(v_b[b][:, :, :, 0:AD + 1],
                                      v_t[:, :, bass.ds(n, 1), :, :].rearrange("p a o h d -> p a (o h) d")).then_inc(vb_ok, 1)

            take_values(0, 0, True)
            take_values(0, 1, True)
            pool.wait_ge(filled, 1)
            def load_part(p):
                heads = bass.ds(p * (H // NP) * HD, H // NP * HD)
                pool.dma_start(raw_q, wq.rearrange("(k p) n -> p k n", p=P)[:, :, heads]).then_inc(ld_wq, 16)
                heads = bass.ds(p * (H // NP), H // NP)
                pool.dma_start(wo_s[:, heads, :], wo.rearrange("(h p) n -> p h n", p=P)[:, heads, :]).then_inc(ld_w, 16)

            def clear_part(p):
                pool.dma_start(xg_blocks[:, bass.ds(p * (BLOCKS // NP), BLOCKS // NP), :],
                              zeros[:].rearrange("p (o d) -> p o d", o=1).broadcast_to([P, BLOCKS // NP, D])).then_inc(cleared, 16)

            others = slice(2, NP)
            pool.wait_ge(ld_k2[1], 16 * J)
            for t in range(TERMS):
                write_term(pool, 2, t, (k_hi, k_hi, k_lo)[t], others, wr_k[1])
            for t in range(TERMS):
                write_term(pool, 1, t, (q_hi, q_lo, q_hi)[t], others, wr_q[1])
            for dst, src in (
                    (gw[:], gate_w.rearrange("(k p) n -> p k n", p=P)),
                    (ffw[:], ff_ln_w.rearrange("(o d) -> o d", o=1).broadcast_to([P, D])),
                    (cos_sin[:], rope), (mask[:], causal), (upp[:], upper), (cst[:], consts)):
                pool.dma_start(dst, src).then_inc(ld_w, 16)
            with nc.allow_non_contiguous_dma(reason="256 weights, one per partition and tile"):
                for k in range(KT):
                    pool.dma_start(lnw[:, k:k + 1], ln_w.rearrange("(k p o) -> k p o", p=P, o=1)[k]).then_inc(ld_w, 16)

            pool.wait_ge(wr_k[1], 2 * TERMS * 16)
            pool.wait_ge(wr_q[1], 2 * TERMS * 16)
            for i, w in enumerate((wk, wv)):
                pool.dma_start(raw_kv[:, :, 512 * i:512 * i + 512], w.rearrange("(k p) n -> p k n", p=P)).then_inc(ld_kv, 16)

            def part_of(w, p):
                return w[:, :, bass.ds(p * (H // NP) * HD, H // NP * HD)]

            def rest_of_part(p):
                pool.wait_ge(whi_ok, p + 1)
                pool.wait_ge(filled, 4)
                nc.gpsimd.tensor_tensor(part_of(wqkv_lo, p), raw_q, part_of(wqkv_hi, p).bitcast(F32),
                                        ALU.subtract).then_inc(wlo_ok, 1)

            def next_part(p):
                rest_of_part(p - 1)
                pool.wait_ge(wlo_ok, p)
                load_part(p)

            load_part(0)
            for b in range(2):
                take_values(1, b)
            pool.wait_ge(ld_kv, 2 * 16)
            nc.gpsimd.tensor_copy(wqkv_hi[:, :, H * HD:], raw_kv).then_inc(whi_kv, 1)
            pool.wait_ge(whi_kv, 1)
            nc.gpsimd.tensor_tensor(wqkv_lo[:, :, H * HD:], raw_kv, wqkv_hi[:, :, H * HD:].bitcast(F32),
                                    ALU.subtract).then_inc(wlo_kv, 1)
            with pool.Fori(2, NP - 1) as p:
                take_values(p, 0)
                next_part(p - 1)
                take_values(p, 1)
                clear_part(p)
            take_values(NP - 1, 0)

            def layernorm_roots(tiles, group):
                pool.wait_ge(var_ok, group)
                nc.gpsimd.tensor_tensor(rstd_b[:, tiles], var_b[:, tiles], mhalf[:, tiles], ALU.pow).then_inc(rstdb_ok, 1)

            def rms_roots(tiles, group):
                pool.wait_ge(msv_ok, group)
                nc.gpsimd.tensor_tensor(rms_b[:, tiles], msv_b[:, tiles], mhalf[:, tiles], ALU.pow).then_inc(rms_ok, 1)

            layernorm_roots(slice(0, EARLY), 1)
            next_part(NP - 2)
            take_values(NP - 1, 1)
            clear_part(NP - 1)
            next_part(NP - 1)
            rms_roots(slice(0, EARLY), 1)
            rest_of_part(NP - 1)

            pool.wait_ge(ot_ok, NP)
            layernorm_roots(slice(EARLY, NP), 2)

            def load_expert(e):
                i = e % 2
                for m, w in enumerate((w1, w3)):
                    pool.dma_start(w13[:, i, :, m, :], w[e].rearrange("(k p) f -> p k f", p=P)).then_inc(ld_e[i], 16)
                pool.dma_start(w2_s[:, i, :, :], w2[e].rearrange("(f p) d -> p f d", p=P)).then_inc(ld_e[i], 16)

            def add_rope(t, c):
                pool.wait_ge(rope_mul, 3 * (GROUPS * t + c + 1))
                heads = slice(4 * c, 4 * c + 4)
                nc.gpsimd.tensor_tensor(rc[:, heads, :], rc[:, heads, :], rs[:, c % 2], ALU.add).then_inc(rope_ok, 1)

            def send(t):
                pool.wait_ge(cleared, 16 * NP)
                pool.wait_ge(routed, R_STEPS * (t + 1))
                nc.gpsimd.tensor_tensor(seen[:], seen[:], chosen[:], ALU.add).then_inc(seen_ok, 1)
                for i in range(2):
                    nc.gpsimd.indirect_dma_start(
                        xg_dram, bass.IndirectOffsetOnAxis(dest[:, i:i + 1], 0), h2_b[:], None).then_inc(sent, 16)

            def inverse_root(t):
                pool.wait_ge(msv2_ok, t + 1)
                nc.gpsimd.tensor_tensor(rms2[:], msv2[:], mhalf[:, 0:1], ALU.pow).then_inc(rms2_ok, 1)

            def step(t):
                fixed = isinstance(t, int)
                if not fixed or t > 0:
                    inverse_root(t - 1)
                if not fixed or t < NP - 1:
                    for c in range(GROUPS):
                        add_rope(t + 1, c)
                if not fixed or t > 0:
                    send(t - 1)

            for c in range(GROUPS):
                add_rope(0, c)
            nc.gpsimd.memset(pr[:], 0.0).then_inc(pr_zero, 1)
            rms_roots(slice(EARLY, NP), 2)
            for p in range(2):
                clear_part(p)
            step(0)
            load_expert(0)
            load_expert(1)
            with pool.Fori(1, NP - 1) as t:
                step(t)
            step(NP - 1)
            inverse_root(NP - 1)
            send(NP - 1)

            pool.wait_ge(table_ok, TABLE_STEPS)
            for e in range(2, E):
                done = pool.value_load(ends_i[0:1, e - 2:e - 1], min_val=1, max_val=N_SLOTS)
                pool.wait_ge(y_ok, done)
                nc.gpsimd.tensor_tensor(freed[:, e:e + 1], ones[:, 0:1], ones[:, 0:1], ALU.mult)
                load_expert(e)
            pool.wait_ge(stores_ok, 4)
            for b in range(2):
                done = pool.value_load(stores[0:1, b:b + 1], min_val=16, max_val=(N_SLOTS + 1) // 2 * 16)
                pool.wait_ge(wr_y[b], done)
                nc.gpsimd.tensor_tensor(freed[:, b:b + 1], ones[:, 0:1], ones[:, 0:1], ALU.mult)
            for t in range(NP):
                for i in range(2):
                    nc.gpsimd.indirect_dma_start(
                        yg[:, i, t, :], None, xg_dram, bass.IndirectOffsetOnAxis(dest_all[:, t, i:i + 1], 0)).then_inc(got[t], 16)

        @block.scalar
        def _(act):
            act.wait_ge(klen_ok, 1)
            nc.scalar.activation(klog[:], klen[:], ACT.Ln).then_inc(klog_ok, 1)
            act.wait_ge(ld_ctx, 16)
            nc.scalar.activation(k_hi[:], ctx_all[:], ACT.Copy).then_inc(khi_ok, 1)
            act.wait_ge(qn_ok, NP)
            nc.scalar.activation(q_hi[:], qn[:], ACT.Copy).then_inc(qhi_ok, 1)
            for g in range(4):
                act.wait_ge(vt_ps, g + 1)
                act.wait_ge(zeroed, ZEROED)
                for half in range(2):
                    nc.scalar.copy(
                        v_t[:, half, 4 * g:4 * g + 4, :, 0:AD].rearrange("p b h d -> p (b h) d"),
                        psum[:, g, 256 * half:256 * half + 256].rearrange("p (n d) -> p n d", d=AD)).then_inc(vt_ok, 1)
            def exps(p, b, first):
                n = 2 * p + b
                if not first:
                    act.wait_ge(pv_ok, n - 1)
                for u in range(8):
                    khalf, j = u // 4, u % 4
                    act.wait_ge(s2_ok, 8 * n + u + 1)
                    nc.scalar.activation(
                        p_t[b][:, khalf, j, :, :],
                        ps_s2[u % 2].rearrange("p (h q) -> p h q", h=HH), ACT.Exp).then_inc(exp_ok, 1)

            def take_out(p, b):
                n = 2 * p + b
                act.wait_ge(pv_ok, n + 1)
                if not isinstance(n, int) or n > 0:
                    act.wait_ge(t_ok, n)
                nc.scalar.copy(o_s[:], ps_o).then_inc(os_ok, 1)

            exps(0, 0, True)
            exps(0, 1, True)

            def part_of(w, p):
                return w[:, :, bass.ds(p * (H // NP) * HD, H // NP * HD)]

            def round_part(p):
                act.wait_ge(ld_wq, 16 * (p + 1))
                act.wait_ge(filled, 4)
                nc.scalar.activation(part_of(wqkv_hi, p), raw_q, ACT.Copy).then_inc(whi_ok, 1)

            act.wait_ge(wr_k[1], 2 * TERMS * 16)
            act.wait_ge(wr_q[1], 2 * TERMS * 16)
            with act.Fori(1, NP) as p:
                for b in range(2):
                    take_out(p - 1, b)
                    exps(p, b, False)
                round_part(p - 1)

            def squares(tiles):
                for t in tiles:
                    act.wait_ge(xr_ok, t + 1)
                    if t:
                        act.wait_ge(sq_ok, t)
                    nc.scalar.activation(sq[:], xr_all[:, t, :], ACT.Square, accum_out=ms_b[:, t:t + 1]).then_inc(sq_ok, 1)

            take_out(NP - 1, 0)
            squares(range(EARLY))
            take_out(NP - 1, 1)
            round_part(NP - 1)

            act.wait_ge(ld_w, LOADS_B * 16)

            def take_h(t, at, last_inc=1):
                act.wait_ge(ring_ok, at + 1)
                for k in range(KT):
                    i = nc.scalar.activation(h_hi[:, k, :], ps_ring[0][:, P * k:P * k + P], ACT.Copy,
                                             scale=lnw[:, k:k + 1])
                i.then_inc(ring_free, last_inc)

            def take_proj(t, c):
                act.wait_ge(proj_ok, (GROUPS + 1) * t + c + 1)
                nc.scalar.copy(raw[:, 4 * c:4 * c + 4, :].rearrange("p h d -> p (h d)"),
                               ps_proj[c % 2]).then_inc(proj_free, 1)

            def take_v(t):
                act.wait_ge(proj_ok, (GROUPS + 1) * (t + 1))
                nc.scalar.copy(v_s[:], ps_proj[GROUPS % 2]).then_inc(proj_free, 1)

            def take_heads(dst, i, at, bank):
                act.wait_ge(ring_ok, at + 1)
                nc.scalar.copy(dst[:, 4 * i:4 * i + 4, :].rearrange("p h n -> p (h n)"),
                               ps_ring[bank]).then_inc(ring_free, 1)

            def take_h2(at, bank, inc=1):
                act.wait_ge(ring_ok, at + inc)
                nc.scalar.copy(h2_t[:].rearrange("p k n -> p (k n)"), ps_ring[bank][:, 0:D]).then_inc(ring_free, inc)

            def step(t):
                fixed = isinstance(t, int)
                first, last = fixed and t == 0, fixed and t == NP - 1
                if not last:
                    take_h(t + 1, ring_at(t, RING_H), 2 if first else 1)
                if not first:
                    square(t - 1)
                for half in range(2):
                    if not last:
                        take_proj(t + 1, half)
                    heads = slice(half * H // 2, (half + 1) * H // 2)
                    act.wait_ge(sub_ok, 2 * t + half + 1)
                    nc.scalar.activation(sc[:, heads, :], sc[:, heads, :], ACT.Exp).then_inc(exps_ok, 1)
                if not last:
                    for c in range(2, 4):
                        take_proj(t + 1, c)
                if not first:
                    take_h2(ring_at(t, RING_L) - (1 if last else 0), RING_L % 3, 2 if last else 1)
                if not last:
                    take_proj(t + 1, 4)
                for i in range(4):
                    take_heads(pr_t, i, ring_at(t, RING_P + i), (RING_P + i) % 3)
                for i in range(4):
                    take_heads(o_t, i, ring_at(t, RING_O + i), (RING_O + i) % 3)
                if not last:
                    take_v(t + 1)
                    for i in range(GROUPS):
                        take_heads(qk_t, i, ring_at(t, RING_T + i), (RING_T + i) % 3)

            def square(t):
                act.wait_ge(x2_ok, t + 1)
                nc.scalar.activation(sq[:], x2[:], ACT.Square, accum_out=ms2[:]).then_inc(sq2_ok, 1)

            take_h(0, 0)
            for c in range(GROUPS):
                take_proj(0, c)
            squares(range(EARLY, NP))
            take_v(0)
            for i in range(GROUPS):
                take_heads(qk_t, i, 1 + i, (1 + i) % 3)
            step(0)
            with act.Fori(1, NP - 1) as t:
                step(t)
            step(NP - 1)
            square(NP - 1)
            take_h2(ring_at(NP - 1, RING_T), RING_T % 3)

            act.wait_ge(table_ok, 1)
            nc.scalar.activation(e21[:], d21[:], ACT.Exp).then_inc(e21_ok, 1)

            def take_xt(s):
                act.wait_ge(xt_ok, s + 1)
                nc.scalar.copy(xs_t[:].rearrange("p k n -> p (k n)"), ps_xt).then_inc(xst_ok, 1)

            def silu(s, part):
                cols = slice(0, FA) if part == 0 else slice(FA, FF)
                act.wait_ge(hid_ok, 4 * s + 2 * part + 1)
                nc.scalar.activation(sil[:, cols], ps_h[part][0][:, 0:cols.stop - cols.start], ACT.Silu).then_inc(silu_ok, 1)

            def take_gt(s, part):
                tiles = slice(0, TA) if part == 0 else slice(TA, FT)
                act.wait_ge(gt_ok, 2 * s + part + 1)
                nc.scalar.copy(g_t[:, tiles, :].rearrange("p f n -> p (f n)"),
                               ps_gt[part][:, 0:P * (tiles.stop - tiles.start)]).then_inc(gts_ok, 1)

            def slot(s, last=False):
                silu(s, 1)
                take_gt(s, 0)
                if not last:
                    take_xt(s + 1)
                take_gt(s, 1)
                if not last:
                    silu(s + 1, 0)

            take_xt(0)
            silu(0, 0)
            with act.Fori(0, N_SLOTS - 1) as s:
                slot(s)
            slot(N_SLOTS - 1, last=True)

        @block.vector
        def _(dve):
            dve.wait_ge(ld_x, 16)
            for p in range(NP):
                nc.vector.bn_stats(st[:, p, :], x_all[:, p, :]).then_inc(stats, 1)
            dve.wait_ge(stats, NP)
            for p in range(NP):
                nc.vector.bn_aggr(mv[:, p, :], st[:, p, :]).then_inc(stats, 1)
            dve.wait_ge(stats, 2 * NP)
            nc.vector.tensor_scalar(veps[:], mv[:, :, 1], EPS, None, ALU.add).then_inc(veps_ok, 1)
            dve.wait_ge(ld_k, 32)
            nc.vector.tensor_copy(klen[:], klen_i[:]).then_inc(klen_ok, 1)
            dve.wait_ge(rstd_ok, 1)
            dve.wait_ge(klog_ok, 1)
            nc.vector.scalar_tensor_tensor(out=rstd_s[:], in0=klog[:], scalar=A_SCALE, in1=rstd[:],
                                           op0=ALU.mult, op1=ALU.mult).then_inc(s_ok, 1)
            dve.wait_ge(s_ok, 1)
            for p in range(NP):
                nc.vector.tensor_scalar(qn[:, p, :], x_all[:, p, :], mv[:, p, 0:1], rstd_s[:, p:p + 1],
                                        ALU.subtract, ALU.mult).then_inc(qn_ok, 1)
            dve.wait_ge(khi_ok, 1)
            dve.wait_ge(ld_ctx, 16)
            nc.vector.tensor_tensor(k_lo[:], ctx_all[:], k_hi[:].bitcast(F32), ALU.subtract).then_inc(klo_ok, 1)
            dve.wait_ge(qhi_ok, 1)
            dve.wait_ge(qn_ok, NP)
            nc.vector.tensor_tensor(q_lo, qn[:], q_hi[:].bitcast(F32), ALU.subtract).then_inc(qlo_ok, 1)

            def maxima(p, b, c, first):
                n = 2 * p + b
                if c == 0 and not first:
                    dve.wait_ge(maxt_ok, n - 1)
                dve.wait_ge(s1_ok, 4 * n + c + 1)
                nc.vector.tensor_reduce(negmax[b][:, c // 2, :, 64 * (c % 2):64 * (c % 2) + 64:32], ps_s1[c % 2], AX.X, ALU.max,
                                        negate=True).then_inc(max_ok, 1)

            def with_max(p, b):
                n = 2 * p + b
                dve.wait_ge(maxt_ok, n + 1)
                dve.wait_ge(ld_q[b], 16 * J * (p + 1))
                nc.vector.tensor_tensor(q_m[b][:], q_b[b][:].bitcast(F32),
                                        ps_max.rearrange("p (h q) -> p h q", h=HH), ALU.add).then_inc(qm_ok, 1)

            def normalise(p, b, first=False):
                n = 2 * p + b
                dve.wait_ge(t_ok, n + 1)
                nc.vector.reciprocal(rsum[:], ps_t[:, :, :, :, AD]).then_inc(rsum_ok, 1)
                dve.wait_ge(rsum_ok, n + 1)
                if b == 0 and not first:
                    dve.wait_ge(ot_ok, p)
                for hh in range(HH):
                    nc.vector.tensor_tensor(
                        a_out[:, :, b, hh], ps_t[:, hh, :, :, 0:AD],
                        rsum[:, hh].rearrange("p a (j o) -> p a j o", o=1).broadcast_to([P, 2, J, AD]),
                        ALU.mult).then_inc(aout_ok, 1)

            def add_x(p):
                dve.wait_ge(ot_ok, p + 1)
                nc.vector.tensor_tensor(x_all[:, bass.ds(p, 1), :].rearrange("p o d -> p (o d)"),
                                        x_all[:, bass.ds(p, 1), :].rearrange("p o d -> p (o d)"),
                                        ps_ot, ALU.add).then_inc(x1_ok, 1)

            def step(p, b):
                n = 2 * p + b
                fixed = isinstance(n, int)
                if not fixed or n < B:
                    with_max(p, b)
                for c in range(4):
                    if not fixed or n + 1 < B:
                        maxima(*ahead(p, b, 1), c, fixed and n + 1 < 2)
                    if c == 1 and (not fixed or n >= 2):
                        normalise(p - 1, b, first=fixed and n == 2)
                if b == 1 and (not fixed or n >= 3):
                    add_x(p - 1)

            dve.wait_ge(zeroed, ZEROED)
            for c in range(4):
                maxima(0, 0, c, True)
            for n in range(4):
                step(n // 2, n % 2)

            with dve.Fori(2, NP - 1) as p:
                for b in range(2):
                    step(p, b)

            def row_stats(tiles):
                done = 2 * tiles.start
                dve.wait_ge(x1_ok, tiles.stop)
                for t in tiles:
                    nc.vector.bn_stats(st_b[:, t, :], x_all[:, t, :]).then_inc(bst_ok, 1)
                dve.wait_ge(bst_ok, done + len(tiles))
                for t in tiles:
                    nc.vector.bn_aggr(mv_b[:, t, :], st_b[:, t, :]).then_inc(bst_ok, 1)
                dve.wait_ge(bst_ok, done + 2 * len(tiles))
                cols = slice(tiles.start, tiles.stop)
                nc.vector.tensor_scalar(var_b[:, cols], mv_b[:, cols, 1], EPS, None, ALU.add).then_inc(var_ok, 1)

            def centre(tiles, group):
                dve.wait_ge(rstdb_ok, group)
                for t in tiles:
                    nc.vector.tensor_scalar(xr_all[:, t, :], x_all[:, t, :], mv_b[:, t, 0:1], rstd_b[:, t:t + 1],
                                            ALU.subtract, ALU.mult).then_inc(xr_ok, 1)

            def mean_squares(tiles):
                dve.wait_ge(sq_ok, tiles.stop)
                cols = slice(tiles.start, tiles.stop)
                nc.vector.tensor_scalar(msv_b[:, cols], ms_b[:, cols], 1.0 / D, EPS, ALU.mult, ALU.add).then_inc(msv_ok, 1)

            row_stats(range(EARLY))
            step(NP - 1, 0)
            step(NP - 1, 1)
            centre(range(EARLY), 1)
            step(NP, 0)
            mean_squares(range(EARLY))
            step(NP, 1)
            dve.wait_ge(rms_ok, 1)
            dve.wait_ge(xr_ok, EARLY)

            def rows(a, t):
                return a[:, bass.ds(t, 1), :].rearrange("p o d -> p (o d)")

            def norm_rows(t):
                if not isinstance(t, int) or t > 0:
                    dve.wait_ge(proj_ok, (GROUPS + 1) * (t - 1) + 1)
                    dve.wait_ge(zeroed, ZEROED)
                nc.vector.tensor_tensor(h_b[:], rows(xr_all, t), rms_b[:, bass.ds(t, 1)].broadcast_to([P, D]),
                                        ALU.mult).then_inc(hb_ok, 1)

            def rest_of_rows(t, at):
                dve.wait_ge(ring_free, at + 1)
                for k in range(KT):
                    nc.vector.scalar_tensor_tensor(
                        out=h_lo[:, k, :], in0=ps_ring[0][:, P * k:P * k + P], scalar=lnw[:, k:k + 1],
                        in1=h_hi[:, k, :].bitcast(F32), op0=ALU.mult, op1=ALU.subtract).then_inc(hlo_ok, 1)

            def rope_products(t, c):
                dve.wait_ge(proj_free, (GROUPS + 1) * t + c + 1)
                if c >= 2:
                    dve.wait_ge(rope_ok, GROUPS * t + c - 1)
                heads = slice(4 * c, 4 * c + 4)
                tables = cos_sin[:].rearrange("p (t o) d -> p t o d", o=1)
                nc.vector.tensor_tensor(rc[:, heads, :], raw[:, heads, :],
                                        tables[:, 0].broadcast_to([P, 4, HD]), ALU.mult).then_inc(rope_mul, 1)
                for i in range(2):
                    nc.vector.tensor_tensor(rs[:, c % 2, :, i::2], raw[:, heads, 1 - i::2],
                                            tables[:, 1, :, i::2].broadcast_to([P, 4, HD // 2]),
                                            ALU.mult).then_inc(rope_mul, 1)

            def per_head(a, half):
                return a[:, half * H // 2:(half + 1) * H // 2]

            def mask_scores(t, half):
                n = 2 * t + half + 1
                sc_half = per_head(sc, half)
                dve.wait_ge(sc_ok, n)
                nc.vector.scalar_tensor_tensor(
                    out=sc_half, in0=per_head(ps_sc, half), scalar=B_SCALE,
                    in1=mask[:].rearrange("p (o k) -> p o k", o=1).broadcast_to([P, H // 2, S]),
                    op0=ALU.mult, op1=ALU.add).then_inc(masked_ok, 1)
                dve.wait_ge(masked_ok, n)
                nc.vector.tensor_reduce(per_head(smax, half), sc_half, AX.X, ALU.max).then_inc(smax_ok, 1)
                dve.wait_ge(smax_ok, n)
                nc.vector.tensor_tensor(
                    sc_half, sc_half, per_head(smax, half).rearrange("p (h o) -> p h o", o=1).broadcast_to([P, H // 2, S]),
                    ALU.subtract).then_inc(sub_ok, 1)

            def probabilities(t, half):
                n = 2 * t + half + 1
                dve.wait_ge(exps_ok, n)
                nc.vector.tensor_reduce(per_head(ssum, half), per_head(sc, half), AX.X, ALU.add).then_inc(ssum_ok, 1)
                dve.wait_ge(ssum_ok, n)
                nc.vector.reciprocal(per_head(srec, half), per_head(ssum, half)).then_inc(srec_ok, 1)
                dve.wait_ge(srec_ok, n)
                for b in range(2):
                    rws = slice(b * S, (b + 1) * S)
                    nc.vector.tensor_tensor(
                        per_head(pr, half)[rws, :, b, :], per_head(sc, half)[rws],
                        per_head(srec, half)[rws].rearrange("p (h o) -> p h o", o=1).broadcast_to([S, H // 2, S]),
                        ALU.mult).then_inc(pr_ok, 1)

            def choose(t):
                def after(i):
                    dve.wait_ge(routed, R_STEPS * t + i)

                dve.wait_ge(lg_ok, t + 1)
                nc.vector.tensor_copy(lg_s[:], ps_lg).then_inc(routed, 1)
                nc.vector.max(mx[:], ps_lg).then_inc(routed, 1)
                after(2)
                nc.vector.tensor_copy(top2[:], mx[:, 0:2]).then_inc(routed, 1)
                nc.vector.max_index(ix[:], mx[:], lg_s[:]).then_inc(routed, 1)
                after(4)
                nc.vector.tensor_copy(ixf[:], ix[:, 0:2]).then_inc(routed, 1)
                dve.wait_ge(zeroed, ZEROED)
                nc.vector.tensor_copy(rows(top_all, t), top2[:]).then_inc(placed, 1)
                after(5)
                nc.vector.tensor_tensor(
                    onehot[:], ixf[:].rearrange("p (i o) -> p i o", o=1).broadcast_to([P, 2, E]),
                    cview("expert", "p (o e) -> p o e", o=1).broadcast_to([P, 2, E]), ALU.is_equal).then_inc(routed, 1)
                after(6)
                if not isinstance(t, int) or t > 0:
                    dve.wait_ge(seen_ok, t)
                nc.vector.tensor_tensor(chosen[:], onehot[:, 0, :], onehot[:, 1, :], ALU.add).then_inc(routed, 1)

            def place(t):
                def after(i):
                    dve.wait_ge(routed, R_STEPS * t + i)

                dve.wait_ge(pos_ok, t + 1)
                nc.vector.tensor_tensor(row_of[:], ps_pos, cview("region_row"), ALU.add).then_inc(routed, 1)
                after(8)
                nc.vector.tensor_tensor(own[:], onehot[:], row_of[:].rearrange("p (o e) -> p o e", o=1).broadcast_to([P, 2, E]),
                                        ALU.mult).then_inc(routed, 1)
                after(9)
                nc.vector.tensor_reduce(dest_f[:], own[:], AX.X, ALU.add).then_inc(routed, 1)
                after(10)
                if not isinstance(t, int) or t > 0:
                    dve.wait_ge(sent, 32 * t)
                nc.vector.tensor_copy(dest[:], dest_f[:]).then_inc(routed, 1)
                dve.wait_ge(zeroed, ZEROED)
                nc.vector.tensor_copy(rows(dest_all, t), dest_f[:]).then_inc(placed, 1)

            def add_residual(t):
                dve.wait_ge(wo_ok, t + 1)
                dve.wait_ge(zeroed, ZEROED)
                nc.vector.tensor_tensor(x2[:], ps_wo, rows(xr_all, t), ALU.add).then_inc(x2_ok, 1)
                dve.wait_ge(x2_ok, t + 1)
                dve.wait_ge(zeroed, ZEROED)
                nc.vector.tensor_tensor(rows(x_all, t), rows(x_all, t), x2[:], ALU.add).then_inc(sum_ok, 1)

            def second_variance(t):
                dve.wait_ge(sq2_ok, t + 1)
                nc.vector.tensor_scalar(msv2[:], ms2[:], 1.0 / D, EPS, ALU.mult, ALU.add).then_inc(msv2_ok, 1)

            def second_norm(t):
                if not isinstance(t, int) or t > 0:
                    dve.wait_ge(sent, 32 * t)
                dve.wait_ge(rms2_ok, t + 1)
                nc.vector.scalar_tensor_tensor(out=h2_b[:], in0=x2[:], scalar=rms2[:, 0:1], in1=ffw[:],
                                               op0=ALU.mult, op1=ALU.mult).then_inc(h2_ok, 1)

            def step(t):
                fixed = isinstance(t, int)
                first, last = fixed and t == 0, fixed and t == NP - 1
                if not last:
                    rest_of_rows(t + 1, ring_at(t, RING_H))
                if not first:
                    second_variance(t - 1)
                mask_scores(t, 0)
                mask_scores(t, 1)
                probabilities(t, 0)
                if not first:
                    second_norm(t - 1)
                probabilities(t, 1)
                if not last:
                    rope_products(t + 1, 0)
                    rope_products(t + 1, 1)
                    rope_products(t + 1, 2)
                    rope_products(t + 1, 3)
                if not first:
                    choose(t - 1)
                if not last:
                    rope_products(t + 1, 4)
                if not first:
                    place(t - 1)
                if not fixed or t + 2 < NP:
                    norm_rows(t + 2)
                add_residual(t)

            norm_rows(0)
            rest_of_rows(0, 0)
            norm_rows(1)
            row_stats(range(EARLY, NP))
            dve.wait_ge(ld_w, LOADS_B * 16)
            rope_products(0, 0)
            rope_products(0, 1)
            centre(range(EARLY, NP), 2)
            for c in range(2, GROUPS):
                rope_products(0, c)
            mean_squares(range(EARLY, NP))
            dve.wait_ge(pr_zero, 1)
            step(0)
            step(1)
            dve.wait_ge(rms_ok, 2)
            dve.wait_ge(xr_ok, NP)
            with dve.Fori(2, NP - 2) as t:
                step(t)
            step(NP - 2)
            step(NP - 1)
            second_variance(NP - 1)
            second_norm(NP - 1)
            choose(NP - 1)
            place(NP - 1)

            def after(i):
                dve.wait_ge(table_ok, i)

            dve.wait_ge(routed, R_STEPS * NP)
            nc.vector.tensor_tensor(d21[:], top_all[:, :, 1], top_all[:, :, 0], ALU.subtract).then_inc(table_ok, 1)
            dve.wait_ge(total_ok, 1)
            nc.vector.tensor_copy(tot[:], ps_pos).then_inc(table_ok, 1)
            after(2)
            nc.vector.tensor_tensor(over[:], tot[:].rearrange("p (e o) -> p e o", o=1).broadcast_to([P, E, REGION - 1]),
                                    cview("steps", "p (e j) -> p e j", e=E), ALU.is_gt).then_inc(table_ok, 1)
            after(3)
            nc.vector.tensor_reduce(n_tiles[:], over[:], AX.X, ALU.add).then_inc(table_ok, 1)
            after(4)
            nc.vector.tensor_scalar(n_tiles[:], n_tiles[:], 1.0, None, ALU.add).then_inc(table_ok, 1)
            nc.vector.tensor_copy(weigh[:, 0:3, :], cview("per_expert", "p (r e) -> p r e", r=3)).then_inc(table_ok, 1)
            after(5)
            nc.vector.tensor_tensor(upto_s[:], n_tiles[:].rearrange("p (o e) -> p o e", o=1).broadcast_to([P, E, E]),
                                    cview("upto", "p (a e) -> p a e", a=E), ALU.mult).then_inc(table_ok, 1)
            nc.vector.tensor_scalar(weigh[:, 3, :], n_tiles[:, 0:E - 1], -1.0, float(REGION),
                                    ALU.mult, ALU.add).then_inc(table_ok, 1)
            after(7)
            nc.vector.tensor_reduce(ends[:], upto_s[:], AX.X, ALU.add).then_inc(table_ok, 1)
            after(9)
            nc.vector.tensor_copy(ends_i[:], ends[:]).then_inc(table_ok, 1)
            nc.vector.tensor_tensor(
                past[:], cview("slot", "p (s o) -> p s o", o=1).broadcast_to([P, N_SLOTS, E - 1]),
                ends[:, 0:E - 1].rearrange("p (o e) -> p o e", o=1).broadcast_to([P, N_SLOTS, E - 1]),
                ALU.is_ge).then_inc(table_ok, 1)
            after(11)
            for r in range(4):
                nc.vector.tensor_tensor(pastw[:, r], past[:], weigh[:, r:r + 1, :].broadcast_to([P, N_SLOTS, E - 1]),
                                        ALU.mult).then_inc(table_ok, 1)
            after(15)
            nc.vector.tensor_reduce(tab_f[:], pastw[:], AX.X, ALU.add).then_inc(table_ok, 1)
            after(16)
            nc.vector.tensor_tensor(tab_f[:], tab_f[:], cview("start", "p (r s) -> p r s", r=4), ALU.add).then_inc(table_ok, 1)
            after(17)
            nc.vector.tensor_copy(tab[:], tab_f[:]).then_inc(table_ok, 1)
            nc.vector.tensor_tensor(
                used[:], ends[:, E - 1:E].rearrange("p (o e) -> p o e", o=1).broadcast_to([P, 2, N_SLOTS]),
                cview("slot", "p (o s) -> p o s", o=1).broadcast_to([P, 2, N_SLOTS]), ALU.is_gt).then_inc(stores_ok, 1)
            dve.wait_ge(stores_ok, 1)
            nc.vector.tensor_tensor(used[:], used[:], cview("store", "p (b s) -> p b s", b=2), ALU.mult).then_inc(stores_ok, 1)
            dve.wait_ge(stores_ok, 2)
            nc.vector.tensor_reduce(stores_f[:], used[:], AX.X, ALU.add).then_inc(stores_ok, 1)
            dve.wait_ge(stores_ok, 3)
            nc.vector.tensor_copy(stores[:], stores_f[:]).then_inc(stores_ok, 1)
            dve.wait_ge(e21_ok, 1)
            nc.vector.tensor_scalar(den[:], e21[:], 1.0, None, ALU.add).then_inc(gates_ok, 1)
            dve.wait_ge(gates_ok, 1)
            nc.vector.reciprocal(gates[:, 0, :], den[:]).then_inc(gates_ok, 1)
            dve.wait_ge(gates_ok, 2)
            nc.vector.tensor_tensor(gates[:, 1, :], e21[:], gates[:, 0, :], ALU.mult).then_inc(gates_ok, 1)

            def products(s, part):
                cols = slice(0, FA) if part == 0 else slice(FA, FF)
                dve.wait_ge(silu_ok, 2 * s + part + 1)
                dve.wait_ge(hid_ok, 4 * s + 2 * part + 2)
                nc.vector.tensor_tensor(g_s[:, cols], sil[:, cols], ps_h[part][1][:, 0:cols.stop - cols.start],
                                        ALU.mult).then_inc(g_ok, 1)

            def take_y(i, b):
                dve.wait_ge(y_ok, 2 * i + b + 1)
                if not isinstance(i, int) or i > 0:
                    dve.wait_ge(wr_y[b], 16 * i)
                nc.vector.tensor_copy(y_s[b][:], ps_y).then_inc(ys_ok, 1)

            def slot(i, b):
                products(2 * i + b, 1)
                if not isinstance(i, int) or 2 * i + b + 1 < N_SLOTS:
                    products(2 * i + b + 1, 0)
                take_y(i, b)

            products(0, 0)
            slot(0, 0)
            slot(0, 1)
            with dve.Fori(1, N_SLOTS // 2) as i:
                for b in range(2):
                    slot(i, b)
            slot(N_SLOTS // 2, 0)

            dve.wait_ge(sum_ok, NP)
            dve.wait_ge(gates_ok, 3)
            for t in range(NP):
                dve.wait_ge(got[t], 32)
                nc.vector.scalar_tensor_tensor(out=mix[:, t, :], in0=yg[:, 0, t, :], scalar=gates[:, 0, t:t + 1],
                                               in1=x_all[:, t, :], op0=ALU.mult, op1=ALU.add).then_inc(mix_ok, 1)
                dve.wait_ge(mix_ok, 2 * t + 1)
                nc.vector.scalar_tensor_tensor(out=mix[:, t, :], in0=yg[:, 1, t, :], scalar=gates[:, 1, t:t + 1],
                                               in1=mix[:, t, :], op0=ALU.mult, op1=ALU.add).then_inc(mix_ok, 1)

        @block.tensor
        def _(pe):
            pe.wait_ge(ld_c, 16)
            pe.wait_ge(ld_ctx, 16)
            for g in range(4):
                for half in range(2):
                    for pp in range(2):
                        i = nc.tensor.transpose(psum[:, g, 256 * half + 128 * pp:256 * half + 128 * pp + 128],
                                                ctx_all[:, 2 * g + pp, 128 * half:128 * half + 128], idn[:])
                i.then_inc(vt_ps, 1)

            def scores_q(p, b, c, first=False):
                n = 2 * p + b
                qhalf, jp = c // 2, c % 2
                if c == 0:
                    pe.wait_ge(ld_k1[b], 16 * J * (p + 1))
                    pe.wait_ge(ld_q[b], 16 * J * (p + 1))
                if not first or c >= 2:
                    pe.wait_ge(max_ok, 4 * n + c - 1)
                for hh in range(HH):
                    i = nc.tensor.matmul(ps_s1[c % 2][:, hh], q_b[b][:, hh, 128 * qhalf:128 * qhalf + 128],
                                         k_1[b][:, hh, 2 * jp:2 * jp + 2, :], start=True, stop=True)
                i.then_inc(s1_ok, 1)

            def max_rows(p, b, first=False):
                n = 2 * p + b
                pe.wait_ge(max_ok, 4 * n + 4)
                if not first:
                    pe.wait_ge(qm_ok, n)
                    if b == 0:
                        pe.wait_ge(x1_ok, p - 1)
                    else:
                        pe.wait_ge(aout_ok, 2 * n - 4)
                for hh in range(HH):
                    for qhalf in range(2):
                        at = D * hh + 128 * qhalf
                        i = nc.tensor.transpose(ps_max[:, at:at + 128], negmax[b][:, qhalf, hh, :], idn[:])
                i.then_inc(maxt_ok, 1)

            def scores_k(p, b, u, first=False):
                n = 2 * p + b
                khalf, j = u // 4, u % 4
                if u == 0:
                    pe.wait_ge(qm_ok, n + 1)
                    pe.wait_ge(ld_k2[b], 16 * J * (p + 1))
                if not first or u >= 2:
                    pe.wait_ge(exp_ok, 8 * n + u - 1)
                for hh in range(HH):
                    i = nc.tensor.matmul(ps_s2[u % 2][:, D * hh:D * (hh + 1)],
                                         k_2[b][:, hh, j, 128 * khalf:128 * khalf + 128],
                                         q_m[b][:, hh, :], start=True, stop=True)
                i.then_inc(s2_ok, 1)

            def values(p, b, c):
                n = 2 * p + b
                if c == 0:
                    pe.wait_ge(exp_ok, 8 * n + 8)
                    pe.wait_ge(vb_ok, n + 1)
                    if not isinstance(n, int) or n > 0:
                        pe.wait_ge(os_ok, n)
                hh, khalf = c // 2, c % 2
                for j in range(J):
                    i = nc.tensor.matmul(ps_o[32 * j:32 * j + 32, hh, :], v_b[b][:, khalf, J * hh + j, :],
                                         p_t[b][:, khalf, j, hh, :], start=khalf == 0, stop=khalf == 1)
                if c == 3:
                    i.then_inc(pv_ok, 1)

            def columns(p, b):
                n = 2 * p + b
                pe.wait_ge(os_ok, n + 1)
                if isinstance(n, int) and n >= B - 2:
                    pe.wait_ge(x1_ok, p)
                    pe.wait_ge(aout_ok, 2 * n)
                for hh in range(HH):
                    for a in range(2):
                        i = nc.tensor.transpose(ps_t[:, hh, a].rearrange("p j e -> p (j e)"),
                                                o_s[:, hh, 128 * a:128 * a + 128], idn[:])
                i.then_inc(t_ok, 1)

            def back_rows(p):
                pe.wait_ge(aout_ok, 4 * p + 4)
                for a in range(2):
                    i = nc.tensor.transpose(ps_ot[:, 128 * a:128 * a + 128],
                                            a_out[:, a].rearrange("p b h j d -> p (b h j d)"), idn[:])
                i.then_inc(ot_ok, 1)

            def step(p, b):
                n = 2 * p + b
                fixed = isinstance(n, int)
                if not fixed or n < B:
                    max_rows(p, b, fixed and n < 4)
                for c in range(4):
                    if not fixed or n + 1 < B:
                        scores_q(*ahead(p, b, 1), c)
                    if not fixed or 1 <= n <= B:
                        values(*ahead(p, b, -1), c)
                    if not fixed or n < B:
                        scores_k(p, b, 2 * c, fixed and n == 0)
                        scores_k(p, b, 2 * c + 1, fixed and n == 0)
                    if c == 0 and (not fixed or n >= 2):
                        columns(p - 1, b)
                if b == 1 and (not fixed or n >= 3):
                    back_rows(p - 1)

            pe.wait_ge(vt_ok, 8)
            pe.wait_ge(zeroed, ZEROED)
            for c in range(4):
                scores_q(0, 0, c, first=True)
            for n in range(4):
                step(n // 2, n % 2)
            with pe.Fori(2, NP - 1) as p:
                for b in range(2):
                    step(p, b)
            for n in range(B - 2, B + 2):
                step(n // 2, n % 2)

            def use_ring(at):
                if not isinstance(at, int) or at >= 3:
                    pe.wait_ge(ring_free, at - 2)

            def rows_t(t, at, inc=1):
                pe.wait_ge(hb_ok, t + 1)
                use_ring(at)
                for k in range(KT):
                    i = nc.tensor.transpose(ps_ring[0][:, P * k:P * k + P], h_b[:, P * k:P * k + P], idn[:])
                i.then_inc(ring_ok, inc)

            def project(t, c):
                n = (GROUPS + 1) * t + c
                if c == 0:
                    pe.wait_ge(hlo_ok, KT * (t + 1))
                if not isinstance(n, int) or n >= 2:
                    pe.wait_ge(proj_free, n - 1)
                cols = slice(512 * c, 512 * c + 512)
                terms = [(h, w[:, k, cols], k) for k in range(KT)
                         for h, w in ((h_hi, wqkv_hi), (h_hi, wqkv_lo), (h_lo, wqkv_hi))]
                for m, (h, w, k) in enumerate(terms):
                    i = nc.tensor.matmul(ps_proj[c % 2], h[:, k, :], w, start=m == 0, stop=m == len(terms) - 1)
                i.then_inc(proj_ok, 1)

            def heads_t(t, c, at, bank):
                pe.wait_ge(rope_ok, GROUPS * t + c + 1)
                use_ring(at)
                for j in range(4):
                    i = nc.tensor.transpose(ps_ring[bank][:, P * j:P * j + P], rc[:, 4 * c + j, :], idn[:])
                i.then_inc(ring_ok, 1)

            def scores(t):
                pe.wait_ge(ring_free, ring_at(t, 0))
                for h in range(H):
                    for b in range(2):
                        cols = slice(b * S, (b + 1) * S)
                        i = nc.tensor.matmul(ps_sc[cols, h, :], qk_t[:, h, cols], qk_t[:, H + h // (H // KVH), cols],
                                             start=True, stop=True)
                    if h % (H // 2) == H // 2 - 1:
                        i.then_inc(sc_ok, 1)

            def h2_rows(t, at, bank, inc=1):
                pe.wait_ge(h2_ok, t + 1)
                use_ring(at)
                for k in range(KT):
                    i = nc.tensor.transpose(ps_ring[bank][:, P * k:P * k + P], h2_b[:, P * k:P * k + P], idn[:])
                i.then_inc(ring_ok, inc)

            def logits(at):
                pe.wait_ge(ring_free, at + 1)
                for k in range(KT):
                    i = nc.tensor.matmul(ps_lg, h2_t[:, k, :], gw[:, k, :], start=k == 0, stop=k == KT - 1)
                i.then_inc(lg_ok, 1)

            def positions(t):
                pe.wait_ge(routed, R_STEPS * t + 7)
                nc.tensor.matmul(ps_pos, upp[:], chosen[:], start=True, stop=False)
                if not isinstance(t, int) or t > 0:
                    pe.wait_ge(seen_ok, t)
                nc.tensor.matmul(ps_pos, ones[:], seen[:], start=False, stop=True).then_inc(pos_ok, 1)

            def attend(t):
                for i in range(4):
                    if i % 2 == 0:
                        pe.wait_ge(pr_ok, 4 * t + i + 2)
                    use_ring(ring_at(t, RING_P + i))
                    for j in range(4):
                        m = nc.tensor.transpose(ps_ring[(RING_P + i) % 3][:, P * j:P * j + P],
                                                pr[:, 4 * i + j].rearrange("p b k -> p (b k)"), idn[:])
                    m.then_inc(ring_ok, 1)
                pe.wait_ge(proj_free, (GROUPS + 1) * (t + 1))
                for i in range(4):
                    use_ring(ring_at(t, RING_O + i))
                    nc.tensor.matmul(ps_ring[(RING_O + i) % 3], v_s[:, HD * i:HD * i + HD],
                                     pr_t[:, 4 * i:4 * i + 4, :].rearrange("p h n -> p (h n)"),
                                     start=True, stop=True).then_inc(ring_ok, 1)

            def project_out(t):
                pe.wait_ge(ring_free, ring_at(t, RING_O + 4))
                if not isinstance(t, int) or t > 0:
                    pe.wait_ge(routed, R_STEPS * t)
                for h in range(H):
                    i = nc.tensor.matmul(ps_wo, o_t[:, h, :], wo_s[:, h, :], start=h == 0, stop=h == H - 1)
                i.then_inc(wo_ok, 1)

            def step(t):
                fixed = isinstance(t, int)
                first, last = fixed and t == 0, fixed and t == NP - 1
                if not last:
                    rows_t(t + 1, ring_at(t, RING_H), 2 if first else 1)
                scores(t)
                if not last:
                    for c in range(4):
                        project(t + 1, c)
                if not first:
                    h2_rows(t - 1, ring_at(t, RING_L), RING_L % 3, 2 if last else 1)
                if not last:
                    project(t + 1, 4)
                if not first:
                    logits(ring_at(t, RING_L))
                if not last:
                    project(t + 1, GROUPS)
                attend(t)
                if not first:
                    positions(t - 1)
                if not last:
                    for c in range(GROUPS):
                        heads_t(t + 1, c, ring_at(t, RING_T + c), (RING_T + c) % 3)
                project_out(t)

            pe.wait_ge(ld_w, LOADS_B * 16)
            pe.wait_ge(filled, 4)
            rows_t(0, 0)
            for c in range(GROUPS + 1):
                if c < 4:
                    pe.wait_ge(wlo_ok, 2 * c + 2)
                elif c == 4:
                    pe.wait_ge(wlo_kv, 1)
                project(0, c)
            for c in range(GROUPS):
                heads_t(0, c, 1 + c, (1 + c) % 3)
            step(0)
            with pe.Fori(1, NP - 1) as t:
                step(t)
            step(NP - 1)
            h2_rows(NP - 1, ring_at(NP - 1, RING_T), RING_T % 3)
            logits(ring_at(NP - 1, RING_T))
            positions(NP - 1)
            pe.wait_ge(seen_ok, NP)
            nc.tensor.matmul(ps_pos, ones[:], seen[:], start=True, stop=True).then_inc(total_ok, 1)

            def slot_value(r, s, least, most):
                return pe.value_load(tab[0:1, r, s], min_val=least, max_val=most)

            def x_t(i, b):
                pe.wait_ge(ld_xs[b], 16 * (i + 1))
                for k in range(KT):
                    m = nc.tensor.transpose(ps_xt[:, P * k:P * k + P], xs[b][:, P * k:P * k + P], idn[:])
                m.then_inc(xt_ok, 1)

            def hidden(s, part, buf, ms=(0, 1)):
                n = FA if part == 0 else FF - FA
                for m in ms:
                    for k in range(KT):
                        i = nc.tensor.matmul(ps_h[part][m][:, 0:n], xs_t[:, k, :],
                                             w13[:, bass.ds(buf, 1), k, m, FA * part:FA * part + n].rearrange("p o f -> p (o f)"),
                                             start=k == 0, stop=k == KT - 1)
                    i.then_inc(hid_ok, 1)

            def slot_values(at):
                return [slot_value(0, at, 0, 1)] + [slot_value(1 + i, at, 48, 48 * E // 2) for i in range(2)]

            def hidden_a(s, buf, due):
                for i in range(2):
                    pe.wait_ge(ld_e[i], due[i])
                pe.wait_ge(xst_ok, s + 1)
                hidden(s, 0, buf)

            def g_transposed(s, part):
                pe.wait_ge(g_ok, 2 * s + part + 1)
                tiles = range(0, TA) if part == 0 else range(TA, FT)
                for f in tiles:
                    at = P * (f - tiles[0])
                    i = nc.tensor.transpose(ps_gt[part][:, at:at + P], g_s[:, P * f:P * f + P], idn[:])
                i.then_inc(gt_ok, 1)

            def outputs(s, part, buf, first=False):
                pe.wait_ge(gts_ok, 2 * s + part + 1)
                if part == 0 and not first:
                    pe.wait_ge(ys_ok, s)
                pe.wait_ge(zeroed, ZEROED)
                for f in (range(0, TA) if part == 0 else range(TA, FT)):
                    i = nc.tensor.matmul(ps_y, g_t[:, f, :],
                                         w2_s[:, bass.ds(buf, 1), f, :].rearrange("p o d -> p (o d)"),
                                         start=f == 0, stop=f == FT - 1)
                if part == 1:
                    i.then_inc(y_ok, 1)

            def slot(i, b):
                s = 2 * i + b
                fixed = isinstance(s, int)
                last = fixed and s == N_SLOTS - 1
                at, following = (slice(s, s + 1), slice(s + 1, s + 2)) if fixed else (bass.ds(s, 1), bass.ds(s + 1, 1))
                buf = slot_value(0, at, 0, 1)
                if not last:
                    next_buf, *due = slot_values(following)
                hidden(s, 1, buf, (0,))
                g_transposed(s, 0)
                hidden(s, 1, buf, (1,))
                if not last:
                    x_t(*ahead(i, b, 1))
                outputs(s, 0, buf, fixed and s == 0)
                g_transposed(s, 1)
                if not last:
                    hidden_a(s + 1, next_buf, due)
                outputs(s, 1, buf)

            x_t(0, 0)
            hidden_a(0, 0, (48, 48))
            pe.wait_ge(table_ok, TABLE_STEPS)
            slot(0, 0)
            slot(0, 1)
            with pe.Fori(1, N_SLOTS // 2) as i:
                for b in range(2):
                    slot(i, b)
            slot(N_SLOTS // 2, 0)


def kernel(**inputs):
    import numpy as np
    import concourse.bacc as bacc
    from concourse.bass_utils import run_bass_kernel_spmd

    nc = bacc.Bacc("TRN2", target_bir_lowering=False, num_devices=1)
    arrays = {}

    def given(name, a):
        a = np.ascontiguousarray(a)
        arrays[f"in_{name}"] = a
        return nc.dram_tensor(f"in_{name}", a.shape, mybir.dt.from_np(a.dtype), kind="ExternalInput").ap()

    out = nc.dram_tensor("out_0", (B, S, D), F32, kind="ExternalOutput").ap()
    angle = np.arange(S, dtype=np.float32)[:, None] * (
        np.float32(1000000.0) ** (-np.arange(0, HD, 2, dtype=np.float32) / np.float32(HD)))[None, :]
    cos, sin = np.cos(angle), np.sin(angle)
    rope = np.stack([np.stack([cos, cos], -1).reshape(S, HD), np.stack([-sin, sin], -1).reshape(S, HD)], 1)
    rope = np.concatenate([rope, rope], 0).astype(np.float32)
    causal = np.where(np.arange(S)[:, None] >= np.arange(S)[None, :], 0.0, MASKED).astype(np.float32)
    weights = [given(k, inputs["L0_ffn_" + k]) for k in
               ("ln_w", "ff_ln_w", "wq", "wk", "wv", "wo", "gate_w", "w1", "w3", "w2")]
    pixart_layer(nc, given("x", inputs["x"]), given("ctx", inputs["ctx_2048"]),
                 given("k_length", inputs["itok_B_779_1933"]), *weights,
                 given("ident", np.eye(P, dtype=np.float32)),
                 given("upper", np.triu(np.ones((P, P), np.float32), 1)),
                 given("rope", rope), given("causal", np.concatenate([causal, causal], 0)),
                 given("consts", const_table(np)), out)
    r = run_bass_kernel_spmd(nc, [arrays], core_ids=[0])
    return r.results[0]["out_0"]
```
